# Optimizing a Trainium2 kernel written in Bass

```python
import numpy as np
import jax
import jax.numpy as jnp

def _softmax(x, axis=-1):
    return jax.nn.softmax(x, axis=axis)

def _gelu(x):
    return jax.nn.gelu(x, approximate=True)

def _silu(x):
    return jax.nn.silu(x)

def _sigmoid(x):
    return jax.nn.sigmoid(x)

def _layernorm(x, axis=-1, eps=1e-05):
    m = jnp.mean(x, axis=axis, keepdims=True)
    v = jnp.var(x, axis=axis, keepdims=True)
    return (x - m) / jnp.sqrt(v + eps)

def _scatter_add(tgt, idx, src, axis=0):
    return tgt.at[idx].add(src)

def _segment_sum(src, seg, n):
    return jax.ops.segment_sum(src, seg, n)
kernel_name = 'mk_flamingo_gated_d1_seqx_r8_a73513'

def setup_inputs(seed: int=0):
    np.random.seed(seed)
    _w = jnp.asarray

    def _rec_inputs():
        import jax
        import jax.numpy as jnp
        _rk = jax.random.key(seed)
        x = -0.0005146 + 1 * jax.random.normal(jax.random.fold_in(_rk, 1), (4, 256, 128), jnp.float32)
        _lenS = 256 - jax.random.randint(jax.random.fold_in(_rk, 7), (4,), 0, max(1, 256 // 4) + 1, jnp.int32)
        _lenS2 = 256 - jax.random.randint(jax.random.fold_in(_rk, 8), (4,), 0, max(1, 256 // 4) + 1, jnp.int32)
        _ctx_768P = jax.random.normal(jax.random.fold_in(_rk, 11), (4, 16, 96), jnp.float32)
        _ctx_768c = jax.random.dirichlet(jax.random.fold_in(_rk, 511), 0.3 * jnp.ones((16,), jnp.float32), (4, 256))
        _ctx_768t = jnp.einsum('bsk,bkd->bsd', _ctx_768c, _ctx_768P)
        _ctx_768t = _ctx_768t * jax.lax.rsqrt(jnp.mean(jnp.square(_ctx_768t)) + 1e-12) * 0.953939
        ctx_768 = -0.00040386 + 0.999972 * (_ctx_768t + 0.3 * jax.random.normal(jax.random.fold_in(_rk, 611), (4, 256, 96), jnp.float32))
        _validS = jnp.arange(256)[None, :] < _lenS[:, None]
        _validS2 = jnp.arange(256)[None, :] < _lenS2[:, None]
        _causal = jnp.tril(jnp.ones((256, 256), dtype=bool))
        mask_BxS2_bk0 = jnp.logical_not(jnp.broadcast_to(_validS2[:, :], (4, 256)))
        _g = jax.random.normal(jax.random.fold_in(_rk, 9001), (2, 1), jnp.float32)
        _g = jnp.sign(_g) * jnp.maximum(jnp.abs(_g), 1.0) + (_g == 0) * 1.0
        g_xattn = _g[0]
        g_ffn = _g[1]
        return (x, ctx_768, mask_BxS2_bk0, g_xattn, g_ffn)
    x, ctx_768, mask_BxS2_bk0, g_xattn, g_ffn = _rec_inputs()

    def _L0_xattn_setup():
        import jax, jax.numpy as jnp
        import numpy as np
        DIM_IN, DIM_LAT, DIM_HEAD = (96, 128, 64)
        INNER = max(DIM_LAT, DIM_IN)
        HEADS = INNER // DIM_HEAD
        SCALE = DIM_HEAD ** (-0.5)
        RMS_EPS = 1e-08
        LN_EPS = 1e-05

        def layernorm(x, g, b):
            mu = jnp.mean(x, axis=-1, keepdims=True)
            var = jnp.mean((x - mu) ** 2, axis=-1, keepdims=True)
            return (x - mu) * jax.lax.rsqrt(var + LN_EPS) * g + b

        def rmsnorm(x, gamma):
            norm = jnp.sqrt(jnp.sum(x * x, axis=-1, keepdims=True)) * x.shape[-1] ** (-0.5)
            return x / jnp.maximum(norm, RMS_EPS) * gamma
        key = jax.random.key(seed)
        ks = jax.random.split(key, 12)
        b, n, m = (4, 512, 64)
        x = jax.random.normal(ks[0], (b, n, DIM_IN), jnp.float32)
        latents = jax.random.normal(ks[1], (b, m, DIM_LAT), jnp.float32)
        mask = jax.random.randint(ks[2], (b, n), 0, 2).astype(bool)
        s = lambda k, sh, fan: jax.random.normal(k, sh, jnp.float32) * fan ** (-0.5)
        return {'x': x, 'latents': latents, 'mask': mask, 'ln_x_g': jnp.ones((DIM_IN,), jnp.float32), 'ln_x_b': jnp.zeros((DIM_IN,), jnp.float32), 'ln_l_g': jnp.ones((DIM_LAT,), jnp.float32), 'ln_l_b': jnp.zeros((DIM_LAT,), jnp.float32), 'qn_g': jnp.ones((DIM_HEAD,), jnp.float32), 'kn_g': jnp.ones((DIM_HEAD,), jnp.float32), 'Wq': s(ks[3], (INNER, DIM_LAT), DIM_LAT), 'Wkv': s(ks[4], (2 * INNER, DIM_IN), DIM_IN), 'Wlkv': s(ks[5], (2 * INNER, DIM_LAT), DIM_LAT), 'Wo': s(ks[6], (DIM_LAT, INNER), INNER), 'bo': jnp.zeros((DIM_LAT,), jnp.float32)}
    _L0_xattn_all = _L0_xattn_setup()
    _L0_xattn_in = {k: v for k, v in _L0_xattn_all.items() if k in ('ln_x_g', 'ln_x_b', 'ln_l_g', 'ln_l_b', 'qn_g', 'kn_g', 'Wq', 'Wkv', 'Wlkv', 'Wo', 'bo')}
    del _L0_xattn_all

    def _L0_ffn_setup():
        import jax, jax.numpy as jnp
        import numpy as np
        DMODEL = 128
        N_EXPERTS = 32
        EXPERT_SIZE = 64
        N_HEADS = 4
        WEIGHT_SCALE = 1.0
        key = jax.random.key(seed)
        k0, k1, k2, k3 = jax.random.split(key, 4)
        x = jax.random.normal(k0, (2, 256, DMODEL), dtype=jnp.float32)
        expert_sel = jax.random.normal(k1, (N_EXPERTS, DMODEL), dtype=jnp.float32) * DMODEL ** (-0.5)
        keys = jax.random.normal(k2, (N_EXPERTS, DMODEL, EXPERT_SIZE), dtype=jnp.float32) * DMODEL ** (-0.5)
        values = jax.random.normal(k3, (N_EXPERTS, EXPERT_SIZE, DMODEL), dtype=jnp.float32) * (N_EXPERTS * EXPERT_SIZE) ** (-0.5)
        return {'x': x, 'expert_sel': expert_sel, 'keys': keys, 'values': values}
    _L0_ffn_all = _L0_ffn_setup()
    _L0_ffn_in = {k: v for k, v in _L0_ffn_all.items() if k in ('expert_sel', 'keys', 'values')}
    del _L0_ffn_all
    return {'x': x, 'ctx_768': ctx_768, 'mask_BxS2_bk0': mask_BxS2_bk0, 'g_xattn': g_xattn, 'g_ffn': g_ffn, 'L0_xattn_ln_x_g': _L0_xattn_in['ln_x_g'], 'L0_xattn_ln_x_b': _L0_xattn_in['ln_x_b'], 'L0_xattn_ln_l_g': _L0_xattn_in['ln_l_g'], 'L0_xattn_ln_l_b': _L0_xattn_in['ln_l_b'], 'L0_xattn_qn_g': _L0_xattn_in['qn_g'], 'L0_xattn_kn_g': _L0_xattn_in['kn_g'], 'L0_xattn_Wq': _L0_xattn_in['Wq'], 'L0_xattn_Wkv': _L0_xattn_in['Wkv'], 'L0_xattn_Wlkv': _L0_xattn_in['Wlkv'], 'L0_xattn_Wo': _L0_xattn_in['Wo'], 'L0_xattn_bo': _L0_xattn_in['bo'], 'L0_ffn_expert_sel': _L0_ffn_in['expert_sel'], 'L0_ffn_keys': _L0_ffn_in['keys'], 'L0_ffn_values': _L0_ffn_in['values']}

def reference(x, ctx_768, mask_BxS2_bk0, g_xattn, g_ffn, L0_xattn_ln_x_g, L0_xattn_ln_x_b, L0_xattn_ln_l_g, L0_xattn_ln_l_b, L0_xattn_qn_g, L0_xattn_kn_g, L0_xattn_Wq, L0_xattn_Wkv, L0_xattn_Wlkv, L0_xattn_Wo, L0_xattn_bo, L0_ffn_expert_sel, L0_ffn_keys, L0_ffn_values):
    import jax
    import jax.numpy as jnp

    def _L0_xattn_ref(x, latents, mask, ln_x_g, ln_x_b, ln_l_g, ln_l_b, qn_g, kn_g, Wq, Wkv, Wlkv, Wo, bo):
        import jax, jax.numpy as jnp
        import numpy as np
        DIM_IN, DIM_LAT, DIM_HEAD = (96, 128, 64)
        INNER = max(DIM_LAT, DIM_IN)
        HEADS = INNER // DIM_HEAD
        SCALE = DIM_HEAD ** (-0.5)
        RMS_EPS = 1e-08
        LN_EPS = 1e-05

        def layernorm(x, g, b):
            mu = jnp.mean(x, axis=-1, keepdims=True)
            var = jnp.mean((x - mu) ** 2, axis=-1, keepdims=True)
            return (x - mu) * jax.lax.rsqrt(var + LN_EPS) * g + b

        def rmsnorm(x, gamma):
            norm = jnp.sqrt(jnp.sum(x * x, axis=-1, keepdims=True)) * x.shape[-1] ** (-0.5)
            return x / jnp.maximum(norm, RMS_EPS) * gamma
        b, n, _ = x.shape
        m = latents.shape[1]
        xn = layernorm(x, ln_x_g, ln_x_b)
        ln = layernorm(latents, ln_l_g, ln_l_b)
        q = ln @ Wq.T
        kv = jnp.concatenate([xn @ Wkv.T, ln @ Wlkv.T], axis=1)
        k, v = (kv[..., :INNER], kv[..., INNER:])
        split_heads = lambda t: t.reshape(t.shape[0], t.shape[1], HEADS, DIM_HEAD).transpose(0, 2, 1, 3)
        q, k, v = (split_heads(q), split_heads(k), split_heads(v))
        qn = rmsnorm(q, qn_g) * SCALE
        kn = rmsnorm(k, kn_g)
        attn = jnp.einsum('bhid,bhjd->bhij', qn, kn)
        full_mask = jnp.pad(mask, ((0, 0), (0, m)), constant_values=True)
        attn = jnp.where(full_mask[:, None, None, :], attn, -jnp.finfo(attn.dtype).max)
        attn = jax.nn.softmax(attn, axis=-1)
        out = jnp.einsum('bhij,bhjd->bhid', attn, v)
        out = out.transpose(0, 2, 1, 3).reshape(b, m, INNER)
        return out @ Wo.T + bo

    def _L0_ffn_ref(x, expert_sel, keys, values):
        import jax, jax.numpy as jnp
        import numpy as np
        DMODEL = 128
        N_EXPERTS = 32
        EXPERT_SIZE = 64
        N_HEADS = 4
        WEIGHT_SCALE = 1.0
        B, S, D = x.shape
        xt = x.reshape(-1, D)
        N = xt.shape[0]
        sel_logits = jnp.einsum('nd,ed->ne', xt, expert_sel)
        gates = jax.nn.sigmoid(sel_logits)
        sel_val, sel_idx = jax.lax.top_k(gates, N_HEADS)
        gate_full = jnp.zeros_like(gates).at[jnp.arange(N)[:, None], sel_idx].set(sel_val)
        scores = jax.nn.relu(jnp.einsum('nd,edf->nef', xt, keys))
        scores = scores * gate_full[:, :, None]
        out = jnp.einsum('nef,efv->nv', scores, values)
        return out.reshape(B, S, -1)
    x = x + jnp.tanh(g_xattn[0]) * _L0_xattn_ref(ctx_768, _layernorm(x, axis=-1), mask_BxS2_bk0, L0_xattn_ln_x_g, L0_xattn_ln_x_b, L0_xattn_ln_l_g, L0_xattn_ln_l_b, L0_xattn_qn_g, L0_xattn_kn_g, L0_xattn_Wq, L0_xattn_Wkv, L0_xattn_Wlkv, L0_xattn_Wo, L0_xattn_bo)
    x = x + jnp.tanh(g_ffn[0]) * _L0_ffn_ref(_layernorm(x, axis=-1), L0_ffn_expert_sel, L0_ffn_keys, L0_ffn_values)
    return x

_drawn_inputs = setup_inputs


def setup_inputs(seed=0):
    import zlib

    import numpy as np

    out = dict(_drawn_inputs(seed))
    spreads = {'L0_xattn_ln_x_g': (1.0, 0.6),
     'L0_xattn_ln_x_b': (0.0, 0.382),
     'L0_xattn_ln_l_g': (1.0, 0.2),
     'L0_xattn_ln_l_b': (0.0, 0.1),
     'L0_xattn_qn_g': (1.0, 0.2),
     'L0_xattn_kn_g': (1.0, 0.2),
     'L0_xattn_bo': (0.0, 0.1)}
    factors = {}
    for name, (base, spread) in spreads.items():
        noise = np.random.default_rng([zlib.crc32(name.encode()), seed]).standard_normal(out[name].shape)
        drawn = base * np.exp(spread * noise) if base else spread * noise
        out[name] = jnp.asarray(drawn.astype(out[name].dtype))
    for name, factor in factors.items():
        out[name] = (out[name] * factor).astype(out[name].dtype)
    return out
```

```python
from contextlib import ExitStack

import numpy as np

import concourse.bass as bass
from concourse import mybir

P = 128
ALU = mybir.AluOpType
ACT = mybir.ActivationFunctionType
F32 = mybir.dt.float32
F32R = mybir.dt.float32r
BF16 = mybir.dt.bfloat16
U8 = mybir.dt.uint8

B, S, D, DC = 4, 256, 128, 96
HEADS, DH = 2, 64
E, F = 32, 64
TOP = 4
SH = 97
EC = E * F // P
NT = B * S // P
BT = S // P
KT = 2 * BT
HALF = 2
HB = B // HALF
HT = NT // HALF
HN = HT * P
G = 6
GR = G - HEADS
NR = KT * HEADS + BT * HEADS
LN_EPS = 1e-5
RMS_EPS = 1e-8
BIG = 2.0 ** 100
SATURATED = 16.6355323
SENTINEL = -3.0e38
TAKEN = -1.0e38
LAG, FIRST_UP, PACE, PACE1, DOWN_LAG = 4.05, 17.5, 0.8, 1, 2
WOA = D + 1

A_LAT, A_CTX = 0, G * DH
A_VEC = A_CTX + 4 * DH
V_LG, V_LB, V_CG, V_CB, V_QG, V_KG, V_GX, V_GF = range(8)
A_COLS = A_VEC + 8
B_WO, B_SEL = 0, HEADS * WOA
B_COLS = B_SEL + E


def schedule():
    def attention(h):
        b0 = HB * h
        units = [(b, a) for b in range(b0, b0 + HB) for a in range(HEADS)]
        yield 0, "stats_in", h
        yield 1, "norm_in", h
        yield 2, "turn_in", h
        yield 3, "project", b0
        yield 3.5, "project", b0 + 1
        yield 4, "norm_qk", h
        yield 5, "turn_qk", h
        yield 6, "row_max", b0
        yield 6.5, "row_max", b0 + 1
        yield 7, "turn_max", h
        for n, unit in enumerate(units):
            yield 8 + n, "weights", unit
            yield 9.2 + n, "attend", unit
        yield 10.8, "out_proj", b0
        yield 12.8, "out_proj", b0 + 1
        yield 14, "norm_mid", h
        yield 15, "turn_mid", h
        yield 16, "select", h
        yield 17, "turn_gates", h

    def experts(h):
        for c in range(EC):
            yield c, "up", (h, c)
            yield c + 1.1, "split", (h, c)
            yield c + DOWN_LAG + 0.2, "down", (h, c)
        yield EC + DOWN_LAG, "finish", h

    places = [(p, 0, s, a) for p, s, a in attention(0)]
    places += [(p + LAG, 1, s, a) for p, s, a in attention(1)]
    places += [(5.5, 3, "split_keys", 0), (7.5, 3, "split_values", 0)]
    places += [(FIRST_UP + PACE * p, 2, s, a) for p, s, a in experts(0)]
    places += [(FIRST_UP + PACE * EC + PACE1 * p, 2, s, a) for p, s, a in experts(1)]
    return [(s, a) for _, _, s, a in sorted(places, key=lambda e: e[:2])]


def gated_block(nc, x_in, ctx_in, wa_in, wb_in, mask_in, keys_in, values_in, out):
    SCHEDULE = schedule()
    with ExitStack() as ctx:
        def sb(name, shape, dt=F32):
            return ctx.enter_context(nc.sbuf_tensor(name, shape, dt))

        def sem(name):
            return ctx.enter_context(nc.semaphore(name))

        x = sb("x", [P, NT, D])
        cx = sb("cx", [P, NT, DC])
        wa = sb("wa", [P, A_COLS])
        wb = sb("wb", [P, B_COLS])
        mask_u8 = sb("mask_u8", [P, B, S], U8)
        keys = sb("keys", [P, EC * P])
        values = sb("values", [P, EC * P])
        ident = sb("ident", [P, P])
        ident_b = sb("ident_b", [P, P], BF16)
        expand = sb("expand", [3 * E, EC * P], BF16)
        shift_l = sb("shift_l", [SH, B, KT * P], BF16)
        shift_r = sb("shift_r", [SH, B, S], BF16)
        mask_b = sb("mask_b", [P, B, KT * P], BF16)
        k_hi, k_lo = sb("k_hi", [P, EC * P], F32R), sb("k_lo", [P, EC * P], F32R)
        v_hi, v_lo = sb("v_hi", [P, EC * P], F32R), sb("v_lo", [P, EC * P], F32R)
        sel_hi, sel_lo = sb("sel_hi", [P, E], F32R), sb("sel_lo", [P, E], F32R)
        tanh_g = sb("tanh_g", [P, 2])
        bn_in = sb("bn_in", [P, HALF, 2 * HT, 6])
        mv_in = sb("mv_in", [P, HALF, 2 * HT, 2])
        var_in = sb("var_in", [P, HALF, 2 * HT])
        ln_in = sb("ln_in", [P, HALF, 2 * HT])
        rs_in = sb("rs_in", [P, HALF, 4, 2 * HT])
        xn = sb("xn", [P, NT, D])
        cn = cx
        xnT = sb("xnT", [P, B, S])
        cnT = sb("cnT", [DC, B, S])
        proj = sb("proj", [P, B, KT, G, DH + 1])
        sq = sb("sq", [P, B, NR, DH])
        ss = sb("ss", [P, B, NR])
        ms = sb("ms", [P, B, NR])
        ln_qk = sb("ln_qk", [P, HALF, HB * NR])
        rs_qk = sb("rs_qk", [P, HALF, 4, HB * NR])
        qk = sq
        kT_hi, kT_lo = sb("kT_hi", [P, B, KT * P], F32R), sb("kT_lo", [P, B, KT * P], F32R)
        qT_hi, qT_lo = sb("qT_hi", [P, B, S], F32R), sb("qT_lo", [P, B, S], F32R)
        gq = sb("gq", [P, 1])
        junk = sb("junk", [P, 2, KT * P], BF16)
        mx = sb("mx", [P, B, BT, HEADS])
        shift_c = sb("shift_c", [P, B, BT, SH], BF16)
        prob = sb("prob", [P, 2, KT, S])
        oT = sb("oT", [DH + 1, 2, HEADS, S])
        rsum = sb("rsum", [P, NT, HEADS])
        rsum_g = sb("rsum_g", [P, NT, HEADS])
        x_mid0 = sb("x_mid0", [P, NT, D])
        x_mid = sb("x_mid", [P, NT, D])
        bn_mid = sb("bn_mid", [P, HALF, HT, 6])
        mv_mid = sb("mv_mid", [P, HALF, HT, 2])
        var_mid = sb("var_mid", [P, HALF, HT])
        ln_mid = sb("ln_mid", [P, HALF, HT])
        rs_mid = sb("rs_mid", [P, HALF, 4, HT])
        xm = xn
        xm_hi, xm_lo = sb("xm_hi", [P, HALF, HN], F32R), sb("xm_lo", [P, HALF, HN], F32R)
        logit = sb("logit", [P, NT, E + 8])
        top = sb("top", [P, NT, 8])
        want = sb("want", [P, NT, 8])
        left = sb("left", [P, NT, E + 8])
        exp_l = keys[:, 3 * HN:3 * HN + NT * E].rearrange("p (t e) -> p t e", t=NT)
        one_e = keys[:, 3 * HN + NT * E:4 * HN].rearrange("p (t e) -> p t e", t=NT)
        sig = sb("sig", [P, NT, E])
        gate = sb("gate", [P, NT, E])
        gate_r = sb("gate_r", [P, NT, E])
        gate_p = sb("gate_p", [P, NT, 3, E], BF16)
        gateT = sb("gateT", [3 * E, HALF, HN], BF16)
        relu = sb("relu", [P, 2, HN])
        hid = keys[:, 0:3 * HN].rearrange("p (i n) -> p i n", i=3)
        hid_hi, hid_lo = sb("hid_hi", [P, 3, HN], F32R), sb("hid_lo", [P, 3, HN], F32R)
        yT = xn[:, :, :].rearrange("p (h t) d -> p h (t d)", h=HALF)
        res = x_mid0

        bank = [ctx.enter_context(nc.psum_tensor(f"bank{i}", [P, 512], F32)) for i in range(8)]
        H_BANK, G_BANK, ACC_BANK = (0, 1), 2, (3, 7)

        in_x = [sem(f"in_x{h}") for h in range(HALF)]
        in_cx = [sem(f"in_cx{h}") for h in range(HALF)]
        in_wa, in_wb, in_mask = sem("in_wa"), sem("in_wb"), sem("in_mask")
        in_keys, in_values = sem("in_keys"), sem("in_values")
        out_done = sem("out_done")
        ident_zero, ident_ready, ident_b_ready = sem("ident_zero"), sem("ident_ready"), sem("ident_b_ready")
        ones_ready, zeros_ready, shift_ready, expand_ready = sem("ones_ready"), sem("zeros_ready"), sem("shift_ready"), sem("expand_ready")
        sentinels_ready = sem("sentinels_ready")
        split_lo = sem("split_lo")
        dve_step = sem("dve_step")
        gq_ready, mask_ready, sel_ready = sem("gq_ready"), sem("mask_ready"), sem("sel_ready")
        var_ready, xn_ready = sem("var_ready"), sem("xn_ready")
        ms_ready, qk_ready = sem("ms_ready"), sem("qk_ready")
        qk_lo_ready = sem("qk_lo_ready")
        max_taken, mx_ready, shift_set = sem("max_taken"), sem("mx_ready"), sem("shift_set")
        mid_ready, var_mid_ready, xm_ready, xm_lo_ready = sem("mid_ready"), sem("var_mid_ready"), sem("xm_ready"), sem("xm_lo_ready")
        logit_ready, gates_ready = sem("logit_ready"), sem("gates_ready")
        hid_ready, hid_lo_ready = sem("hid_ready"), sem("hid_lo_ready")
        res_ready = sem("res_ready")
        split_hi, squares_ready, hid_hi_ready = sem("split_hi"), sem("squares_ready"), sem("hid_hi_ready")
        tanh_ready, act_step = sem("tanh_ready"), sem("act_step")
        y0_in, y0_qk, y0_mid = sem("y0_in"), sem("y0_qk"), sem("y0_mid")
        inT_ready, proj_ready, qk_hi_ready = sem("inT_ready"), sem("proj_ready"), sem("qk_hi_ready")
        prob_ready, oT_ready = sem("prob_ready"), sem("oT_ready")
        xm_hi_ready, exp_ready, gateT_ready = sem("xm_hi_ready"), sem("exp_ready"), sem("gateT_ready")
        relu_ready, yT_ready = sem("relu_ready"), sem("yT_ready")
        inT_done, proj_done, qkT_done = sem("inT_done"), sem("proj_done"), sem("qkT_done")
        max_done, mxT_done, score_done = sem("max_done"), sem("mxT_done"), sem("score_done")
        attend_done, out_done_pe, xmT_done = sem("attend_done"), sem("out_done_pe"), sem("xmT_done")
        logit_done, gateT_done = sem("logit_done"), sem("gateT_done")
        up_done, spread_done, down_done, resT_done = sem("up_done"), sem("spread_done"), sem("down_done"), sem("resT_done")

        def vec(v):
            return wa[:, A_VEC + v:A_VEC + v + 1]

        block = ctx.enter_context(nc.Block())

        @block.sync
        def _(sp):
            for h in range(HALF):
                t = slice(HT * h, HT * h + HT)
                sp.dma_start(x[:, t, :], x_in[:, t, :]).then_inc(in_x[h], 16)
                sp.dma_start(cx[:, t, :], ctx_in[:, t, :]).then_inc(in_cx[h], 16)
                if h == 0:
                    sp.dma_start(wa[:, :], wa_in).then_inc(in_wa, 16)
                    sp.dma_start(mask_u8[:, :, :].rearrange("p b s -> p (b s)"),
                                 mask_in.to_broadcast([P, B * S])).then_inc(in_mask, 16)
            sp.dma_start(wb[:, :], wb_in).then_inc(in_wb, 16)
            sp.dma_start(keys[:, :], keys_in).then_inc(in_keys, 16)
            sp.dma_start(values[:, :], values_in).then_inc(in_values, 16)
            for h in range(HALF):
                t = slice(HT * h, HT * h + HT)
                sp.wait_ge(res_ready, h + 1)
                sp.dma_start(out[:, t, :], res[:, t, :]).then_inc(out_done, 16)
            sp.wait_ge(out_done, 16 * HALF)

        @block.gpsimd
        def _(pool):
            pool.memset(ident[:, :], 0.0).then_inc(ident_zero, 1)
            pool.wait_ge(ident_zero, 1)
            pool.affine_select(out=ident[:, :], in_=ident[:, :], compare_op=ALU.not_equal, fill=1.0, base=0,
                               pattern=[[-1, P]], channel_multiplier=1).then_inc(ident_ready, 1)
            for b in range(B):
                pool.memset(proj[:, b, :, G - HEADS:G, DH:DH + 1], 1.0).then_inc(ones_ready, 1)
            pool.memset(shift_l[:, :, :], 1.0).then_inc(zeros_ready, 1)
            pool.memset(mask_b[:, :, S:], 0.0).then_inc(zeros_ready, 1)
            pool.memset(shift_c[:, :, :, :], 0.0).then_inc(zeros_ready, 1)
            pool.wait_ge(zeros_ready, 3)
            pool.memset(shift_c[:, :, :, 32:SH:64], 1.0).then_inc(shift_ready, 1)
            pool.memset(ident_b[:, :], 0.0).then_inc(ident_zero, 1)
            pool.wait_ge(ident_zero, 2)
            pool.affine_select(out=ident_b[:, :], in_=ident_b[:, :], compare_op=ALU.not_equal, fill=1.0, base=0,
                               pattern=[[-1, P]], channel_multiplier=1).then_inc(ident_b_ready, 1)
            pool.memset(logit[:, :, E:], SENTINEL).then_inc(sentinels_ready, 1)
            pool.memset(want[:, :, TOP:], SENTINEL).then_inc(sentinels_ready, 1)

            def background():
                pool.memset(expand[:, :], 0.0).then_inc(expand_ready, 1)
                for i in range(3):
                    pool.wait_ge(expand_ready, i + 1)
                    pool.affine_select(out=expand[:, :], in_=expand[:, :], compare_op=ALU.not_equal, fill=1.0,
                                       base=-E * i, pattern=[[-1, E], [0, F]], channel_multiplier=1).then_inc(expand_ready, 1)
                for n, (src, hi, lo) in enumerate(((keys, k_hi, k_lo), (values, v_hi, v_lo))):
                    pool.wait_ge(split_hi, n + 1)
                    pool.tensor_tensor(lo[:, :], src[:, :], hi[:, :].bitcast(F32), ALU.subtract).then_inc(split_lo, 1)

            background()

        @block.vector
        def _(dve):
            steps = [0]

            def then(ins):
                steps[0] += 1
                ins.then_inc(dve_step, 1)
                dve.wait_ge(dve_step, steps[0])

            def newton(y, v, w):
                then(dve.scalar_tensor_tensor(w[:, 1, :], y, -0.5, y, ALU.mult, ALU.mult))
                then(dve.tensor_tensor(w[:, 2, :], w[:, 1, :], v, ALU.mult))
                then(dve.scalar_tensor_tensor(w[:, 3, :], w[:, 2, :], 1.5, y, ALU.add, ALU.mult))

            def stats_in(h):
                dve.wait_ge(in_x[h], 16)
                for j in range(HT):
                    dve.bn_stats(bn_in[:, h, j, :], x[:, HT * h + j, :])
                dve.wait_ge(in_cx[h], 16)
                for j in range(HT):
                    last = dve.bn_stats(bn_in[:, h, HT + j, :], cx[:, HT * h + j, :])
                then(last)
                for j in range(2 * HT):
                    last = dve.bn_aggr(mv_in[:, h, j, :], bn_in[:, h, j, :])
                then(last)
                dve.tensor_scalar(var_in[:, h, 0:HT], mv_in[:, h, 0:HT, 1], 1.0 + LN_EPS, LN_EPS * LN_EPS,
                                  ALU.mult, ALU.add)
                dve.tensor_scalar(var_in[:, h, HT:], mv_in[:, h, HT:, 1], LN_EPS, None, ALU.add).then_inc(var_ready, 1)

            def norm_in(h):
                dve.wait_ge(var_ready, h + 1)
                dve.wait_ge(y0_in, h + 1)
                newton(rs_in[:, h, 0, :], var_in[:, h, :], rs_in[:, h, :, :])
                for j in range(HT):
                    last = dve.tensor_scalar(xn[:, HT * h + j, :], x[:, HT * h + j, :], mv_in[:, h, j, 0:1],
                                             rs_in[:, h, 3, j:j + 1], ALU.subtract, ALU.mult)
                    last = dve.tensor_scalar(cn[:, HT * h + j, :], cx[:, HT * h + j, :], mv_in[:, h, HT + j, 0:1],
                                             rs_in[:, h, 3, HT + j:HT + j + 1], ALU.subtract, ALU.mult)
                    last.then_inc(xn_ready, 1)
                if h == 0:
                    dve.wait_ge(in_mask, 16)
                    dve.wait_ge(zeros_ready, 3)
                    dve.tensor_scalar(mask_b[:, :, 0:S], mask_u8[:, :, :], BIG, -BIG, ALU.mult, ALU.add).then_inc(mask_ready, 1)
                    dve.wait_ge(mask_ready, 1)
                    for row in range(32, SH, DH):
                        dve.tensor_copy(shift_l[row:row + 1, :, :], mask_b[row:row + 1, :, :]).then_inc(mask_ready, 1)
                    dve.wait_ge(in_wa, 16)
                    dve.tensor_scalar(gq[:, :], vec(V_QG), float(DH) ** -0.5, None, ALU.mult).then_inc(gq_ready, 1)
                    dve.wait_ge(gq_ready, 1)

            def norm_qk(h):
                for b in range(HB * h, HB * h + HB):
                    dve.wait_ge(squares_ready, 3 * (b + 1))
                    last = dve.tensor_reduce(ss[:, b, :], sq[:, b, :, :], mybir.AxisListType.X, ALU.add)
                then(last)
                bb = slice(HB * h, HB * h + HB)
                dve.tensor_scalar(ms[:, bb, :], ss[:, bb, :], 1.0 / DH, RMS_EPS * RMS_EPS, ALU.mult, ALU.max).then_inc(ms_ready, 1)
                dve.wait_ge(ms_ready, h + 1)
                dve.wait_ge(y0_qk, h + 1)
                newton(rs_qk[:, h, 0, :], ms[:, bb, :].rearrange("p b r -> p (b r)"), rs_qk[:, h, :, :])
                for b in range(HB * h, HB * h + HB):
                    r0 = NR * (b - HB * h)
                    for lo, hi, src, n in ((0, KT * HEADS, proj[:, b, :, 2:4, 0:DH], KT),
                                           (KT * HEADS, NR, proj[:, b, BT:, 0:2, 0:DH], BT)):
                        r = rs_qk[:, h, 3, r0 + lo:r0 + hi].rearrange("p (t a) -> p t a", t=n).unsqueeze(3)
                        dve.tensor_tensor(qk[:, b, lo:hi, :].rearrange("p (t a) d -> p t a d", t=n), src,
                                          r.to_broadcast([P, n, HEADS, DH]), ALU.mult).then_inc(qk_ready, 1)

            def turn_qk(h):
                for b in range(HB * h, HB * h + HB):
                    dve.wait_ge(qk_hi_ready, 2 * b + 1)
                    dve.scalar_tensor_tensor(kT_lo[:, b, :], bank[4 * h + 2 * (b % HB)][:, :], vec(V_KG),
                                             kT_hi[:, b, :].bitcast(F32), ALU.mult, ALU.subtract).then_inc(qk_lo_ready, 1)
                    dve.wait_ge(qk_hi_ready, 2 * b + 2)
                    dve.scalar_tensor_tensor(qT_lo[:, b, :], bank[4 * h + 2 * (b % HB) + 1][:, 0:S], gq[:, :],
                                             qT_hi[:, b, :].bitcast(F32), ALU.mult, ALU.subtract).then_inc(qk_lo_ready, 1)

            def row_max(b):
                h = b // HB
                for i in range(BT * HEADS):
                    n = BT * HEADS * b + i
                    dve.wait_ge(max_done, n + 1)
                    if n >= 2:
                        dve.wait_ge(max_taken, n - 1)
                    dve.tensor_tensor_reduce(junk[:, n % 2, :], bank[4 * h + i][:, :], mask_b[:, b, :], 1.0, SENTINEL,
                                             ALU.add, ALU.max, mx[:, b, i // HEADS, i % HEADS:i % HEADS + 1]).then_inc(max_taken, 1)
                if b % HB < HB - 1:
                    return
                dve.wait_ge(max_taken, BT * HEADS * (b + 1))
                bb = slice(HB * h, HB * h + HB)
                if h == 0:
                    dve.wait_ge(shift_ready, 1)
                dve.tensor_scalar(shift_c[:, bb, :, 0:SH:DH], mx[:, bb, :, :], -1.0, None, ALU.mult).then_inc(mx_ready, 1)

            def turn_max(h):
                for b in range(HB * h, HB * h + HB):
                    dve.wait_ge(mxT_done, b + 1)
                    dve.tensor_copy(shift_r[:, b, :], bank[4 * h + b % HB][0:SH, :].bitcast(BF16)[:, 0:S]).then_inc(shift_set, 1)

            def out_proj(b):
                h = b // HB
                for t in range(BT):
                    j = BT * b + t
                    dve.wait_ge(out_done_pe, j + 1)
                    last = dve.reciprocal(rsum[:, j, :],
                                          bank[4 * h + t][:, 0:2 * WOA].rearrange("p (a n) -> p a n", a=HEADS)[:, :, D])
                then(last)
                if b == 0:
                    dve.wait_ge(tanh_ready, 1)
                then(dve.tensor_scalar(rsum_g[:, BT * b:BT * b + BT, :], rsum[:, BT * b:BT * b + BT, :], tanh_g[:, 0:1],
                                       None, ALU.mult))
                for t in range(BT):
                    j = BT * b + t
                    last = dve.scalar_tensor_tensor(x_mid0[:, j, :], bank[4 * h + t][:, 0:D], rsum_g[:, j, 0:1],
                                                    x[:, j, :], ALU.mult, ALU.add)
                then(last)
                for t in range(BT):
                    j = BT * b + t
                    dve.scalar_tensor_tensor(x_mid[:, j, :], bank[4 * h + t][:, WOA:WOA + D], rsum_g[:, j, 1:2],
                                             x_mid0[:, j, :], ALU.mult, ALU.add).then_inc(mid_ready, 1)

            def norm_mid(h):
                dve.wait_ge(mid_ready, HT * (h + 1))
                for j in range(HT):
                    last = dve.bn_stats(bn_mid[:, h, j, :], x_mid[:, HT * h + j, :])
                then(last)
                for j in range(HT):
                    last = dve.bn_aggr(mv_mid[:, h, j, :], bn_mid[:, h, j, :])
                then(last)
                dve.tensor_scalar(var_mid[:, h, :], mv_mid[:, h, :, 1], LN_EPS, None, ALU.add).then_inc(var_mid_ready, 1)
                dve.wait_ge(var_mid_ready, h + 1)
                dve.wait_ge(y0_mid, h + 1)
                newton(rs_mid[:, h, 0, :], var_mid[:, h, :], rs_mid[:, h, :, :])
                for j in range(HT):
                    dve.tensor_scalar(xm[:, HT * h + j, :], x_mid[:, HT * h + j, :], mv_mid[:, h, j, 0:1],
                                      rs_mid[:, h, 3, j:j + 1], ALU.subtract, ALU.mult).then_inc(xm_ready, 1)
                if h == 0:
                    dve.wait_ge(in_wb, 16)
                    dve.tensor_copy(sel_hi[:, :], wb[:, B_SEL:B_SEL + E]).then_inc(sel_ready, 1)
                    dve.wait_ge(sel_ready, 1)
                    dve.tensor_tensor(sel_lo[:, :], wb[:, B_SEL:B_SEL + E], sel_hi[:, :].bitcast(F32),
                                      ALU.subtract).then_inc(sel_ready, 1)

            def turn_mid(h):
                dve.wait_ge(xm_hi_ready, h + 1)
                dve.tensor_tensor(xm_lo[:, h, :], bank[4 * h + 2][:, :], xm_hi[:, h, :].bitcast(F32),
                                  ALU.subtract).then_inc(xm_lo_ready, 1)

            def select(h):
                t = slice(HT * h, HT * h + HT)
                tiles = range(HT * h, HT * h + HT)
                if h == 0:
                    dve.wait_ge(sentinels_ready, 2)
                dve.wait_ge(logit_done, h + 1)
                dve.tensor_scalar(logit[:, t, 0:E], bank[4 * h + 3][:, 0:HT * E].rearrange("p (t e) -> p t e", t=HT),
                                  SATURATED, None, ALU.min).then_inc(logit_ready, 1)
                dve.wait_ge(logit_ready, h + 1)
                for j in tiles:
                    last = dve.max(top[:, j, :], logit[:, j, 0:E])
                then(last)
                then(dve.tensor_copy(want[:, t, 0:TOP], top[:, t, 0:TOP]))
                for j in tiles:
                    last = dve.match_replace(left[:, j, :], want[:, j, :], logit[:, j, :], SENTINEL)
                dve.wait_ge(exp_ready, h + 1)
                then(dve.tensor_scalar(one_e[:, t, :], exp_l[:, t, :], 1.0, None, ALU.add))
                then(dve.reciprocal(sig[:, t, :], one_e[:, t, :]))
                then(dve.scalar_tensor_tensor(gate[:, t, :], left[:, t, 0:E], TAKEN, sig[:, t, :], ALU.is_lt, ALU.mult))
                then(dve.tensor_copy(gate_p[:, t, 0, :], gate[:, t, :]))
                then(dve.tensor_tensor(gate_r[:, t, :], gate[:, t, :], gate_p[:, t, 0, :], ALU.subtract))
                then(dve.tensor_copy(gate_p[:, t, 1, :], gate_r[:, t, :]))
                dve.tensor_tensor(gate_p[:, t, 2, :], gate_r[:, t, :], gate_p[:, t, 1, :], ALU.subtract).then_inc(gates_ready, 1)

            def up(h, c):
                n = EC * h + c
                dve.wait_ge(relu_ready, n + 1)
                dve.wait_ge(spread_done, n + 1)
                if n >= 3:
                    dve.wait_ge(hid_hi_ready, n - 2)
                    dve.wait_ge(hid_lo_ready, n - 2)
                dve.tensor_tensor(hid[:, n % 3, :], bank[G_BANK][:, :], relu[:, n % 2, :], ALU.mult).then_inc(hid_ready, 1)

            def split(h, c):
                n = EC * h + c
                dve.wait_ge(hid_ready, n + 1)
                dve.wait_ge(hid_hi_ready, n + 1)
                if n >= 3:
                    dve.wait_ge(down_done, n - 2)
                dve.tensor_tensor(hid_lo[:, n % 3, :], hid[:, n % 3, :], hid_hi[:, n % 3, :].bitcast(F32),
                                  ALU.subtract).then_inc(hid_lo_ready, 1)

            def finish(h):
                t = slice(HT * h, HT * h + HT)
                dve.wait_ge(resT_done, h + 1)
                dve.scalar_tensor_tensor(res[:, t, :].rearrange("p t d -> p (t d)"), bank[ACC_BANK[h]][:, :],
                                         tanh_g[:, 1:2], x_mid[:, t, :].rearrange("p t d -> p (t d)"),
                                         ALU.mult, ALU.add).then_inc(res_ready, 1)

            run = {"stats_in": stats_in, "norm_in": norm_in, "norm_qk": norm_qk, "turn_qk": turn_qk,
                   "row_max": row_max, "turn_max": turn_max, "split": lambda at: split(*at),
                   "out_proj": out_proj, "norm_mid": norm_mid, "turn_mid": turn_mid, "select": select,
                   "up": lambda at: up(*at), "finish": finish}
            for stage, at in SCHEDULE:
                if stage in run:
                    run[stage](at)

        @block.scalar
        def _(act):
            steps = [0]

            def start_rsqrt(y0, ln, v, ready):
                steps[0] += 1
                act.activation(ln, v, ACT.Ln).then_inc(act_step, 1)
                act.wait_ge(act_step, steps[0])
                act.activation(y0, ln, ACT.Exp, scale=-0.5).then_inc(ready, 1)

            def stats_in(h):
                if h == 0:
                    act.wait_ge(in_wa, 16)
                    act.activation(tanh_g[:, :], wa[:, A_VEC + V_GX:A_VEC + V_GF + 1], ACT.Tanh).then_inc(tanh_ready, 1)
                    act.preload_act_table_set("natural_log_exp_and_others")
                act.wait_ge(var_ready, h + 1)
                start_rsqrt(rs_in[:, h, 0, :], ln_in[:, h, :], var_in[:, h, :], y0_in)

            def turn_in(h):
                for b in range(HB * h, HB * h + HB):
                    bk = bank[4 * h + b % HB]
                    act.wait_ge(inT_done, b + 1)
                    act.activation(xnT[:, b, :], bk[:, 0:S], ACT.Identity, bias=vec(V_LB), scale=vec(V_LG)).then_inc(inT_ready, 1)
                    act.activation(cnT[:, b, :], bk[0:DC, S:2 * S], ACT.Identity, bias=vec(V_CB)[0:DC], scale=vec(V_CG)[0:DC]).then_inc(inT_ready, 1)

            def project(b):
                h = b // HB
                for i in range(3):
                    n = 3 * b + i
                    bk = bank[4 * h + (n - 3 * HB * h + 2) % 4]
                    act.wait_ge(proj_done, n + 1)
                    if i < BT:
                        src = bk[:, 0:G * DH].rearrange("p (g d) -> p g d", g=G)
                        dst = proj[:, b, BT + i, :, 0:DH]
                        act.activation(sq[:, b, HEADS * (BT + i):HEADS * (BT + i + 1), :], src[:, 2:4, :], ACT.Square)
                        act.activation(sq[:, b, HEADS * (KT + i):HEADS * (KT + i + 1), :], src[:, 0:2, :],
                                       ACT.Square).then_inc(squares_ready, 1)
                    else:
                        src = bk[:, :].rearrange("p (t g d) -> p t g d", t=BT, g=4)
                        dst = proj[:, b, 0:BT, 2:G, 0:DH]
                        act.activation(sq[:, b, 0:HEADS * BT, :].rearrange("p (t a) d -> p t a d", t=BT), src[:, :, 0:2, :],
                                       ACT.Square).then_inc(squares_ready, 1)
                    act.activation(dst, src, ACT.Copy).then_inc(proj_ready, 1)

            def split_weights(n, src, hi, arrived):
                act.wait_ge(arrived, 16)
                act.activation(hi[:, :], src[:, :], ACT.Copy).then_inc(split_hi, 1)

            def norm_qk(h):
                act.wait_ge(ms_ready, h + 1)
                bb = slice(HB * h, HB * h + HB)
                start_rsqrt(rs_qk[:, h, 0, :], ln_qk[:, h, :], ms[:, bb, :].rearrange("p b r -> p (b r)"), y0_qk)

            def turn_qk(h):
                if h == 0:
                    act.wait_ge(gq_ready, 1)
                for b in range(HB * h, HB * h + HB):
                    act.wait_ge(qkT_done, 2 * b + 1)
                    act.activation(kT_hi[:, b, :], bank[4 * h + 2 * (b % HB)][:, :], ACT.Copy, scale=vec(V_KG)).then_inc(qk_hi_ready, 1)
                    act.wait_ge(qkT_done, 2 * b + 2)
                    act.activation(qT_hi[:, b, :], bank[4 * h + 2 * (b % HB) + 1][:, 0:S], ACT.Copy, scale=gq[:, :]).then_inc(qk_hi_ready, 1)

            def weights(b, a):
                h, n = b // HB, HEADS * b + a
                for i in range(2):
                    act.wait_ge(score_done, 2 * n + i + 1)
                    if n >= 2 and i == 0:
                        act.wait_ge(attend_done, n - 1)
                    act.activation(prob[:, n % 2, 2 * i:2 * i + 2, :], bank[4 * h + 2 + i][:, :].rearrange("p (t s) -> p t s", t=2),
                                   ACT.Exp).then_inc(prob_ready, 1)

            def attend(b, a):
                h, n = b // HB, HEADS * b + a
                act.wait_ge(attend_done, n + 1)
                if b >= 2:
                    act.wait_ge(out_done_pe, BT * (b - 1))
                act.activation(oT[:, b % 2, a, :], bank[4 * h + a][0:DH + 1, 0:S], ACT.Copy).then_inc(oT_ready, 1)

            def norm_mid(h):
                act.wait_ge(var_mid_ready, h + 1)
                start_rsqrt(rs_mid[:, h, 0, :], ln_mid[:, h, :], var_mid[:, h, :], y0_mid)

            def turn_mid(h):
                act.wait_ge(xmT_done, h + 1)
                act.activation(xm_hi[:, h, :], bank[4 * h + 2][:, :], ACT.Copy).then_inc(xm_hi_ready, 1)

            def select(h):
                t = slice(HT * h, HT * h + HT)
                if h == 0:
                    act.wait_ge(split_lo, 1)
                act.wait_ge(logit_ready, h + 1)
                act.activation(exp_l[:, t, :], logit[:, t, 0:E], ACT.Exp, scale=-1.0).then_inc(exp_ready, 1)

            def turn_gates(h):
                act.wait_ge(gateT_done, h + 1)
                act.activation(gateT[:, h, :], bank[4 * h][0:3 * E, :].bitcast(BF16)[:, 0:HN], ACT.Copy).then_inc(gateT_ready, 1)

            def up(h, c):
                n = EC * h + c
                act.wait_ge(up_done, n + 1)
                if n >= 2:
                    act.wait_ge(hid_ready, n - 1)
                act.activation(relu[:, n % 2, :], bank[H_BANK[n % 2]][:, :], ACT.Relu).then_inc(relu_ready, 1)

            def split(h, c):
                n = EC * h + c
                act.wait_ge(hid_ready, n + 1)
                if n >= 3:
                    act.wait_ge(down_done, n - 2)
                act.activation(hid_hi[:, n % 3, :], hid[:, n % 3, :], ACT.Copy).then_inc(hid_hi_ready, 1)

            def finish(h):
                act.wait_ge(down_done, EC * (h + 1))
                act.activation(yT[:, h, :], bank[ACC_BANK[h]][:, :], ACT.Copy).then_inc(yT_ready, 1)

            run = {"stats_in": stats_in, "turn_in": turn_in, "project": project, "norm_qk": norm_qk, "turn_qk": turn_qk,
                   "split_keys": lambda at: split_weights(0, keys, k_hi, in_keys),
                   "split_values": lambda at: split_weights(1, values, v_hi, in_values), "split": lambda at: split(*at),
                   "weights": lambda at: weights(*at), "attend": lambda at: attend(*at), "norm_mid": norm_mid,
                   "turn_mid": turn_mid, "select": select, "turn_gates": turn_gates,
                   "up": lambda at: up(*at), "finish": finish}
            for stage, at in SCHEDULE:
                if stage in run:
                    run[stage](at)

        @block.tensor
        def _(pe):
            def product(o, lhs, rhs, start, stop):
                (lh, ll), (rh, rl) = lhs, rhs
                pe.matmul(o, ll, rh, start=start, stop=False)
                pe.matmul(o, lh, rl, start=False, stop=False)
                return pe.matmul(o, lh, rh, start=False, stop=stop)

            def turn_in(h):
                if h == 0:
                    pe.wait_ge(ident_ready, 1)
                for b in range(HB * h, HB * h + HB):
                    bk = bank[4 * h + b % HB]
                    pe.wait_ge(xn_ready, BT * (b + 1))
                    for t in range(BT):
                        pe.transpose(bk[:, P * t:P * t + P], xn[:, BT * b + t, :], ident[:, :])
                    for t in range(BT):
                        last = pe.transpose(bk[0:DC, S + P * t:S + P * t + P], cn[:, BT * b + t, :], ident[:, :])
                    last.then_inc(inT_done, 1)

            def project(b):
                h = b // HB
                if b == 0:
                    pe.wait_ge(in_wa, 16)
                for i in range(3):
                    n = 3 * b + i
                    k = n - 3 * HB * h
                    bk = bank[4 * h + (k + 2) % 4]
                    pe.wait_ge(inT_ready, 2 * (b + 1))
                    if k == 2:
                        pe.wait_ge(inT_ready, 2 * (HB * h + 1))
                    if k == 3:
                        pe.wait_ge(inT_ready, 2 * (HB * h + 2))
                    if k >= 4:
                        pe.wait_ge(proj_ready, n - 3)
                    if i < BT:
                        last = pe.matmul(bk[:, 0:G * DH], xnT[:, b, P * i:P * i + P], wa[:, A_LAT:A_LAT + G * DH],
                                         start=True, stop=True)
                    else:
                        for t in range(BT):
                            last = pe.matmul(bk[:, 4 * DH * t:4 * DH * (t + 1)], cnT[:, b, P * t:P * t + P],
                                             wa[0:DC, A_CTX:A_CTX + 4 * DH], start=True, stop=True)
                    last.then_inc(proj_done, 1)

            def turn_qk(h):
                pe.wait_ge(proj_ready, 3 * HB * (h + 1))
                for b in range(HB * h, HB * h + HB):
                    pe.wait_ge(qk_ready, 2 * (b + 1))
                    for kind, tiles, first in ((0, KT, 0), (1, BT, KT)):
                        bk = bank[4 * h + 2 * (b % HB) + kind]
                        for t in range(tiles):
                            src = qk[:, b, HEADS * (first + t):HEADS * (first + t + 1), :].rearrange("p a d -> p (a d)")
                            last = pe.transpose(bk[:, P * t:P * t + P], src, ident[:, :])
                        last.then_inc(qkT_done, 1)

            def row_max(b):
                h = b // HB
                if b % HB == 0:
                    pe.wait_ge(qk_lo_ready, 2 * HB * (h + 1))
                    pe.wait_ge(qk_hi_ready, 2 * HB * (h + 1))
                for i in range(BT * HEADS):
                    n, t, a = BT * HEADS * b + i, i // HEADS, i % HEADS
                    if b % HB:
                        pe.wait_ge(max_taken, n - BT * HEADS + 1)
                    rows = slice(DH * a, DH * a + DH)
                    pe.matmul(bank[4 * h + i][:, :], qT_hi[rows, b, P * t:P * t + P], kT_hi[rows, b, :],
                              start=True, stop=True).then_inc(max_done, 1)

            def turn_max(h):
                if h == 0:
                    pe.wait_ge(ident_b_ready, 1)
                pe.wait_ge(mx_ready, h + 1)
                for b in range(HB * h, HB * h + HB):
                    bk = bank[4 * h + b % HB][0:SH, :].bitcast(BF16)
                    for t in range(BT):
                        last = pe.transpose(bk[:, P * t:P * t + P], shift_c[:, b, t, :], ident_b[:, :])
                    last.then_inc(mxT_done, 1)

            def weights(b, a):
                h, n = b // HB, HEADS * b + a
                if n == 0:
                    pe.wait_ge(mask_ready, 1 + HEADS)
                if (b % HB, a) == (0, 0):
                    pe.wait_ge(shift_set, HB * (h + 1))
                rows = slice(DH * a, DH * a + DH)
                for i in range(2):
                    bk = bank[4 * h + 2 + i]
                    if (b % HB, a) != (0, 0):
                        pe.wait_ge(prob_ready, 2 * (n - 1) + i + 1)
                    for t in range(2 * i, 2 * i + 2):
                        o = bk[:, S * (t % 2):S * (t % 2) + S]
                        keys_t = slice(P * t, P * t + P)
                        pe.matmul(o, shift_l[DH * a:DH * a + 33, b, keys_t], shift_r[DH * a:DH * a + 33, b, :], start=True, stop=False)
                        last = product(o, (kT_hi[rows, b, keys_t], kT_lo[rows, b, keys_t]),
                                       (qT_hi[rows, b, :], qT_lo[rows, b, :]), False, True)
                    last.then_inc(score_done, 1)

            def attend(b, a):
                h, n = b // HB, HEADS * b + a
                if n == 0:
                    pe.wait_ge(ones_ready, B)
                if b % HB:
                    pe.wait_ge(mid_ready, BT * b)
                pe.wait_ge(prob_ready, 2 * n + 2)
                for t in range(KT):
                    last = pe.matmul(bank[4 * h + a][0:DH + 1, 0:S], proj[:, b, t, 4 + a, :], prob[:, n % 2, t, :],
                                     start=(t == 0), stop=(t == KT - 1))
                last.then_inc(attend_done, 1)

            def out_proj(b):
                h = b // HB
                if b == 0:
                    pe.wait_ge(in_wb, 16)
                pe.wait_ge(oT_ready, HEADS * (b + 1))
                for t in range(BT):
                    for a in range(HEADS):
                        last = pe.matmul(bank[4 * h + t][:, WOA * a:WOA * a + WOA], oT[:, b % 2, a, P * t:P * t + P],
                                         wb[0:DH + 1, B_WO + WOA * a:B_WO + WOA * a + WOA], start=True, stop=True)
                    last.then_inc(out_done_pe, 1)

            def turn_mid(h):
                pe.wait_ge(prob_ready, 2 * HEADS * HB * (h + 1))
                for j in range(HT * h, HT * h + HT):
                    pe.wait_ge(xm_ready, j + 1)
                    t = j - HT * h
                    last = pe.transpose(bank[4 * h + 2][:, P * t:P * t + P], xm[:, j, :], ident[:, :])
                last.then_inc(xmT_done, 1)

            def select(h):
                if h == 0:
                    pe.wait_ge(sel_ready, 2)
                pe.wait_ge(xm_hi_ready, h + 1)
                pe.wait_ge(xm_lo_ready, h + 1)
                for t in range(HT):
                    tt = slice(P * t, P * t + P)
                    last = product(bank[4 * h + 3][:, E * t:E * t + E], (xm_hi[:, h, tt], xm_lo[:, h, tt]),
                                   (sel_hi[:, :], sel_lo[:, :]), True, True)
                last.then_inc(logit_done, 1)

            def turn_gates(h):
                pe.wait_ge(gates_ready, h + 1)
                bk = bank[4 * h][0:3 * E, :].bitcast(BF16)
                for t in range(HT):
                    src = gate_p[:, HT * h + t, :, :].rearrange("p i e -> p (i e)")
                    last = pe.transpose(bk[:, P * t:P * t + P], src, ident_b[:, :])
                last.then_inc(gateT_done, 1)

            def up(h, c):
                n = EC * h + c
                cc = slice(P * c, P * c + P)
                if n == 0:
                    pe.wait_ge(split_lo, 1)
                    pe.wait_ge(expand_ready, 4)
                if c == 0:
                    pe.wait_ge(gateT_ready, h + 1)
                if n >= 2:
                    pe.wait_ge(relu_ready, n - 1)
                product(bank[H_BANK[n % 2]][:, :], (k_hi[:, cc], k_lo[:, cc]), (xm_hi[:, h, :], xm_lo[:, h, :]),
                        True, True).then_inc(up_done, 1)
                if n >= 1:
                    pe.wait_ge(hid_ready, n)
                pe.matmul(bank[G_BANK][:, :], expand[:, cc], gateT[:, h, :], start=True, stop=True).then_inc(spread_done, 1)

            def down(h, c):
                n = EC * h + c
                cc = slice(P * c, P * c + P)
                if n == 0:
                    pe.wait_ge(split_lo, 2)
                pe.wait_ge(hid_hi_ready, n + 1)
                pe.wait_ge(hid_lo_ready, n + 1)
                last = product(bank[ACC_BANK[h]][:, :], (v_hi[:, cc], v_lo[:, cc]),
                               (hid_hi[:, n % 3, :], hid_lo[:, n % 3, :]), c == 0, c == EC - 1)
                last.then_inc(down_done, 1)

            def finish(h):
                pe.wait_ge(yT_ready, h + 1)
                for t in range(HT):
                    last = pe.transpose(bank[ACC_BANK[h]][:, P * t:P * t + P], yT[:, h, P * t:P * t + P], ident[:, :])
                last.then_inc(resT_done, 1)

            run = {"turn_in": turn_in, "project": project, "turn_qk": turn_qk, "row_max": row_max, "turn_max": turn_max,
                   "weights": lambda at: weights(*at), "attend": lambda at: attend(*at), "out_proj": out_proj,
                   "turn_mid": turn_mid, "select": select, "turn_gates": turn_gates,
                   "up": lambda at: up(*at), "down": lambda at: down(*at), "finish": finish}
            for stage, at in SCHEDULE:
                if stage in run:
                    run[stage](at)


def kernel(**inputs):
    import concourse.bacc as bacc
    from concourse.bass_utils import run_bass_kernel_spmd

    a = {k: np.asarray(v) for k, v in inputs.items()}
    f32 = np.float32

    def tiles(t):
        return np.ascontiguousarray(t.reshape(NT, P, t.shape[-1]).transpose(1, 0, 2))

    wa = np.zeros((P, A_COLS), f32)
    wa[:, 0:P] = a["L0_xattn_Wq"].T
    wa[:, P:A_CTX] = a["L0_xattn_Wlkv"].T
    wa[0:DC, A_CTX:A_VEC] = a["L0_xattn_Wkv"].T
    wa[:, A_VEC + V_LG] = a["L0_xattn_ln_l_g"]
    wa[:, A_VEC + V_LB] = a["L0_xattn_ln_l_b"]
    wa[0:DC, A_VEC + V_CG] = a["L0_xattn_ln_x_g"]
    wa[0:DC, A_VEC + V_CB] = a["L0_xattn_ln_x_b"]
    for h in range(HEADS):
        wa[DH * h:DH * h + DH, A_VEC + V_QG] = a["L0_xattn_qn_g"]
        wa[DH * h:DH * h + DH, A_VEC + V_KG] = a["L0_xattn_kn_g"]
    wa[:, A_VEC + V_GX] = a["g_xattn"]
    wa[:, A_VEC + V_GF] = a["g_ffn"]
    wb = np.zeros((P, B_COLS), f32)
    for h in range(HEADS):
        wb[0:DH, WOA * h:WOA * h + D] = a["L0_xattn_Wo"][:, DH * h:DH * h + DH].T
        wb[DH, WOA * h + D] = 1.0
    wb[:, B_SEL:B_SEL + E] = a["L0_ffn_expert_sel"].T
    wb[DH, 0:D] = a["L0_xattn_bo"]

    arrays = {
        "x_in": tiles(a["x"]),
        "ctx_in": tiles(a["ctx_768"]),
        "wa_in": wa,
        "wb_in": wb,
        "mask_in": np.ascontiguousarray(a["mask_BxS2_bk0"]).reshape(1, B * S),
        "keys_in": np.ascontiguousarray(a["L0_ffn_keys"].transpose(1, 0, 2).reshape(D, E * F)),
        "values_in": np.ascontiguousarray(a["L0_ffn_values"].reshape(EC, P, D).transpose(1, 0, 2).reshape(P, EC * D)),
    }
    nc = bacc.Bacc("TRN2", target_bir_lowering=False, num_devices=1)
    args = [nc.dram_tensor(n, v.shape, mybir.dt.from_np(v.dtype), kind="ExternalInput").ap() for n, v in arrays.items()]
    out = nc.dram_tensor("out", (P, NT, D), F32, kind="ExternalOutput").ap()
    gated_block(nc, *args, out)
    got = run_bass_kernel_spmd(nc, [arrays], core_ids=[0]).results[0]["out"]
    return np.ascontiguousarray(got.transpose(1, 0, 2)).reshape(B, S, D)
```

```python
from contextlib import ExitStack

import numpy as np

import concourse.bass as bass
from concourse import mybir

P = 128
ALU = mybir.AluOpType
ACT = mybir.ActivationFunctionType
F32 = mybir.dt.float32
F32R = mybir.dt.float32r
BF16 = mybir.dt.bfloat16
U8 = mybir.dt.uint8

B, S, D, DC = 4, 256, 128, 96
HEADS, DH = 2, 64
E, F = 32, 64
TOP = 4
SH = 97
EC = E * F // P
QUARTER = EC * P // 4
WARM_UP = 6
DOWN = 3
RING = DOWN + 1
NT = B * S // P
BT = S // P
KT = 2 * BT
HALF = 2
HB = B // HALF
HT = NT // HALF
HN = HT * P
G = 6
GR = G - HEADS
NR = KT * HEADS + BT * HEADS
LN_EPS = 1e-5
RMS_EPS = 1e-8
BIG = 2.0 ** 100
SATURATED = 16.6355323
SENTINEL = -3.0e38
TAKEN = -1.0e38
WOA = D + 1

ATTENTION = [("turn_in", None), ("project", None), ("sum_qk", None), ("norm_qk", None), ("turn_qk", None),
             ("row_max", None), ("turn_max", None), ("weights", 0), ("attend", 0), ("weights", 1), ("attend", 1),
             ("out_proj", None), ("stats_mid", None), ("norm_mid", None), ("turn_mid", None), ("select", None), ("turn_gates", None)]
IN_PLACES = [[-543.241, -258.091], [-378.79, -166.019], [-339.971, -130.296], [-81.8897, 110.217]]
WARM_PLACES = []
PLACES = [
    [-491.406, -354.1, -273.032, -418.509, -236.595, -185.233, -76.0302, -35.416, -5.47608, 118.407, 157.028, 298.147, 327.504, 376.018, 501.986, 671.633, 850.716],
    [-353.134, -261.566, -228.599, -301.894, -35.8191, 6.62616, 106.068, 131, 296.501, 341.067, 412.632, 442.056, 491.391, 515.952, 679.496, 687.905, 877.981],
    [-185.191, -89.3395, -13.7008, -55.858, 110.791, 354.934, 426.766, 487.851, 544.169, 668.673, 813.022, 941.611, 987.02, 1073.38, 1111.19, 1276.63, 1383.08],
    [-22.02, 65.7721, 145.829, 14.5685, 349.865, 507.256, 641.304, 679.593, 818.438, 888.455, 968.32, 1017.16, 1164.07, 1186.28, 1302.44, 1393.22, 1497.1],
]
SPLIT_PLACES = [[-267.054, 38.3093, 49.8367, 109.844], [153.553, 171.188, 217.332, 259.6]]
CHUNK_PLACES = [
    [917.155, 1063.77, 1183.75, 1410.6, 1640.2],
    [1671.89, 1910.53, 2039.89, 2181.25, 2197.94],
]
LAG = {
    "PE": {"attend": -0.7987, "down": 16.59, "finish": 73.12, "norm_in": 5.489, "norm_mid": -4.257, "norm_qk": -0.4149, "out_proj": -2.438, "project": 0.03959, "row_max": 1.114, "select": 2.358, "split": -1.012, "split_keys": -0.4576, "stats_in": 2.075, "stats_mid": -17.14, "sum_qk": 0.3238, "turn_gates": 1.222, "turn_in": -0.5132, "turn_max": 1.379, "turn_mid": 1.356, "turn_qk": 0.8433, "up": 0.1196, "weights": 5.452},
    "DVE": {"down": -0.4008, "finish": 46.48, "norm_in": -176.5, "norm_mid": -6.494, "norm_qk": 146.1, "out_proj": -2.255, "project": 0.2724, "row_max": -25.88, "select": -0.8155, "split": -0.08659, "split_keys": 3.641, "split_values": -0.0105, "stats_in": 0.9918, "stats_mid": -27.33, "sum_qk": -42.4, "turn_gates": -0.3188, "turn_in": -0.0725, "turn_max": -1.692, "turn_mid": -1.297, "turn_qk": 0.1072, "up": -5.633, "weights": 7.886},
    "ACT": {"attend": -1.373, "finish": 0.000834, "norm_in": -0.9793, "norm_mid": -4.801, "norm_qk": -1.195, "out_proj": -1.785, "project": -6.103, "select": -3.82, "split": 0.3931, "split_keys": 0.4152, "stats_mid": -2.302, "sum_qk": 0.5775, "turn_gates": 2.282, "turn_in": 2.712, "turn_max": -0.3197, "up": -2.094},
}

A_LAT, A_CTX = 0, G * DH
A_VEC = A_CTX + 4 * DH
V_LG, V_LB, V_CG, V_CB, V_QG, V_KG, V_GX, V_GF = range(8)
A_COLS = A_VEC + 8
B_WO, B_SEL = 0, HEADS * WOA
B_COLS = B_SEL + E


def schedule(engine):
    places = [(p, s, b) for b in range(B) for s, p in zip(("stats_in", "norm_in"), IN_PLACES[b])]
    for b in range(B):
        places += [(p, s, b if a is None else (b, a)) for (s, a), p in zip(ATTENTION, PLACES[b])]
    places += [(p, s, q) for s, row in zip(("split_keys", "split_values"), SPLIT_PLACES) for q, p in enumerate(row)]
    places += [(p, "keep_warm", None) for p in WARM_PLACES]
    for h in range(HALF):
        place = np.interp(np.arange(EC + DOWN), np.arange(5) * (EC + DOWN) / 4, CHUNK_PLACES[h])
        for c in range(EC):
            places += [(place[c], "up", (h, c)), (place[c + 1] + 0.001, "split", (h, c)), (place[c + DOWN] + 0.002, "down", (h, c))]
        places += [(CHUNK_PLACES[h][-1], "finish", h)]
    return [(s, a) for _, s, a in sorted(places, key=lambda e: e[0] + LAG[engine].get(e[1], 0))]


def gated_block(nc, x_in, ctx_in, wa_in, wb_in, mask_in, keys_in, values_in, out):
    with ExitStack() as ctx:
        def sb(name, shape, dt=F32):
            return ctx.enter_context(nc.sbuf_tensor(name, shape, dt))

        def sem(name):
            return ctx.enter_context(nc.semaphore(name))

        x = sb("x", [P, NT, D])
        cx = sb("cx", [P, NT, DC])
        wa = sb("wa", [P, A_COLS])
        wb = sb("wb", [P, B_COLS])
        mask_u8 = sb("mask_u8", [P, B, S], U8)
        keys = sb("keys", [P, EC * P])
        values = sb("values", [P, EC * P])
        ident = sb("ident", [P, P])
        ident_b = sb("ident_b", [P, P], BF16)
        expand = sb("expand", [3 * E, EC * P], BF16)
        shift_l = sb("shift_l", [SH, B, KT * P], BF16)
        shift_r = sb("shift_r", [SH, B, S], BF16)
        mask_b = sb("mask_b", [P, B, KT * P], BF16)
        k_hi, k_lo = sb("k_hi", [P, EC * P], F32R), sb("k_lo", [P, EC * P], F32R)
        v_hi, v_lo = sb("v_hi", [P, EC * P], F32R), sb("v_lo", [P, EC * P], F32R)
        sel_hi, sel_lo = sb("sel_hi", [P, E], F32R), sb("sel_lo", [P, E], F32R)
        tanh_g = sb("tanh_g", [P, 2])
        bn_in = sb("bn_in", [P, B, KT, 6])
        mv_in = sb("mv_in", [P, B, KT, 2])
        var_in = sb("var_in", [P, B, KT])
        ln_in = sb("ln_in", [P, B, KT])
        rs_in = sb("rs_in", [P, B, 4, KT])
        xn = sb("xn", [P, NT, D])
        cn = cx
        xnT = sb("xnT", [P, B, S])
        cnT = sb("cnT", [DC, B, S])
        proj = sb("proj", [P, B, KT, G, DH + 1])
        sq = sb("sq", [P, B, NR, DH])
        ss = sb("ss", [P, B, NR])
        ms = sb("ms", [P, B, NR])
        ln_qk = sb("ln_qk", [P, B, NR])
        rs_qk = sb("rs_qk", [P, B, 4, NR])
        qk = sq
        kT_hi, kT_lo = sb("kT_hi", [P, B, KT * P], F32R), sb("kT_lo", [P, B, KT * P], F32R)
        qT_hi, qT_lo = sb("qT_hi", [P, B, S], F32R), sb("qT_lo", [P, B, S], F32R)
        gq = sb("gq", [P, 1])
        junk = sb("junk", [P, 2, KT * P], BF16)
        mx = sb("mx", [P, B, BT, HEADS])
        shift_c = sb("shift_c", [P, B, BT, SH], BF16)
        prob = sb("prob", [P, 2, KT, S])
        oT = sb("oT", [DH + 1, 2, HEADS, S])
        rsum = sb("rsum", [P, NT, HEADS])
        rsum_g = sb("rsum_g", [P, NT, HEADS])
        x_mid0 = sb("x_mid0", [P, NT, D])
        x_mid = sb("x_mid", [P, NT, D])
        bn_mid = sb("bn_mid", [P, B, BT, 6])
        mv_mid = sb("mv_mid", [P, B, BT, 2])
        var_mid = sb("var_mid", [P, B, BT])
        ln_mid = sb("ln_mid", [P, B, BT])
        rs_mid = sb("rs_mid", [P, B, 4, BT])
        xm = xn
        xm_hi, xm_lo = sb("xm_hi", [P, B, S], F32R), sb("xm_lo", [P, B, S], F32R)
        logit = sb("logit", [P, NT, E + 8])
        top = sb("top", [P, NT, 8])
        want = sb("want", [P, NT, 8])
        left = sb("left", [P, NT, E + 8])
        exp_l = keys[:, 3 * HN:3 * HN + NT * E].rearrange("p (t e) -> p t e", t=NT)
        one_e = keys[:, 3 * HN + NT * E:4 * HN].rearrange("p (t e) -> p t e", t=NT)
        sig = sb("sig", [P, NT, E])
        gate = sb("gate", [P, NT, E])
        gate_r = sb("gate_r", [P, NT, E])
        gate_p = sb("gate_p", [P, NT, 3, E], BF16)
        gateT = sb("gateT", [3 * E, B, S], BF16)
        relu = values[:, 0:2 * HN].rearrange("p (i n) -> p i n", i=2)
        hid = keys[:, 0:3 * HN].rearrange("p (i n) -> p i n", i=3)
        hid_hi, hid_lo = sb("hid_hi", [P, RING, HN], F32R), sb("hid_lo", [P, RING, HN], F32R)
        yT = xn[:, :, :].rearrange("p (h t) d -> p h (t d)", h=HALF)
        res = x_mid0

        bank = [ctx.enter_context(nc.psum_tensor(f"bank{i}", [P, 512], F32)) for i in range(8)]
        H_BANK, G_BANK, ACC_BANK = (0, 1), 2, (3, 7)
        TURN_IN, PROJECT, TURN_QK, ROW_MAX, TURN_MAX, UNITS, OUT, TURN_MID, SELECT, TURN_GATES = 0, 1, 4, 6, 10, 11, 17, 19, 20, 21

        def bank_of(b, use):
            return bank[2 * b + use % 2]


        LOADS = (slice(0, BT), slice(BT, 2 * BT), slice(2 * BT, NT))
        in_x = [sem(f"in_x{i}") for i in range(len(LOADS))]
        in_cx = [sem(f"in_cx{i}") for i in range(len(LOADS))]
        in_wa, in_wb, in_mask = sem("in_wa"), sem("in_wb"), sem("in_mask")
        in_keys, in_values = sem("in_keys"), sem("in_values")
        out_done = sem("out_done")
        ident_zero, ident_ready, ident_b_ready = sem("ident_zero"), sem("ident_ready"), sem("ident_b_ready")
        ones_ready, zeros_ready, shift_ready, expand_ready = sem("ones_ready"), sem("zeros_ready"), sem("shift_ready"), sem("expand_ready")
        sentinels_ready = sem("sentinels_ready")
        split_lo, pool_step, parts_ready = sem("split_lo"), sem("pool_step"), sem("parts_ready")
        dve_step = sem("dve_step")
        gq_ready, mask_ready, sel_ready = sem("gq_ready"), sem("mask_ready"), sem("sel_ready")
        var_ready, xn_ready = sem("var_ready"), sem("xn_ready")
        ms_ready, qk_ready = sem("ms_ready"), sem("qk_ready")
        qk_lo_ready = sem("qk_lo_ready")
        max_taken, mx_ready, shift_set = sem("max_taken"), sem("mx_ready"), sem("shift_set")
        mid_ready, var_mid_ready, xm_ready, xm_lo_ready = sem("mid_ready"), sem("var_mid_ready"), sem("xm_ready"), sem("xm_lo_ready")
        logit_ready, gates_ready = sem("logit_ready"), sem("gates_ready")
        hid_ready, hid_lo_ready = sem("hid_ready"), sem("hid_lo_ready")
        res_ready = sem("res_ready")
        keys_hi_ready, values_hi_ready = sem("keys_hi_ready"), sem("values_hi_ready")
        squares_ready, hid_hi_ready = sem("squares_ready"), sem("hid_hi_ready")
        tanh_ready, act_step = sem("tanh_ready"), sem("act_step")
        y0_in, y0_qk, y0_mid = sem("y0_in"), sem("y0_qk"), sem("y0_mid")
        inT_ready, proj_ready, qk_hi_ready = sem("inT_ready"), sem("proj_ready"), sem("qk_hi_ready")
        prob_ready, oT_ready = sem("prob_ready"), sem("oT_ready")
        xm_hi_ready, exp_ready, gateT_ready = sem("xm_hi_ready"), sem("exp_ready"), sem("gateT_ready")
        relu_ready, yT_ready = sem("relu_ready"), sem("yT_ready")
        inT_done, proj_done, qkT_done = sem("inT_done"), sem("proj_done"), sem("qkT_done")
        max_done, mxT_done, score_done = sem("max_done"), sem("mxT_done"), sem("score_done")
        attend_done, out_done_pe, xmT_done = sem("attend_done"), sem("out_done_pe"), sem("xmT_done")
        logit_done, gateT_done = sem("logit_done"), sem("gateT_done")
        up_done, spread_done, down_done, resT_done = sem("up_done"), sem("spread_done"), sem("down_done"), sem("resT_done")

        def vec(v):
            return wa[:, A_VEC + v:A_VEC + v + 1]

        block = ctx.enter_context(nc.Block())

        @block.sync
        def _(sp):
            for i, t in enumerate(LOADS):
                sp.dma_start(x[:, t, :], x_in[:, t, :]).then_inc(in_x[i], 16)
                sp.dma_start(cx[:, t, :], ctx_in[:, t, :]).then_inc(in_cx[i], 16)
                if i == 0:
                    sp.dma_start(wa[:, :], wa_in).then_inc(in_wa, 16)
                if i == 1:
                    sp.dma_start(mask_u8[:, :, :].rearrange("p b s -> p (b s)"),
                                 mask_in.to_broadcast([P, B * S])).then_inc(in_mask, 16)
            sp.dma_start(wb[:, :], wb_in).then_inc(in_wb, 16)
            sp.dma_start(keys[:, :], keys_in).then_inc(in_keys, 16)
            sp.dma_start(values[:, :], values_in).then_inc(in_values, 16)
            for h in range(HALF):
                t = slice(HT * h, HT * h + HT)
                sp.wait_ge(res_ready, h + 1)
                sp.dma_start(out[:, t, :], res[:, t, :]).then_inc(out_done, 16)
            sp.wait_ge(out_done, 16 * HALF)

        @block.gpsimd
        def _(pool):
            pool.memset(ident[:, :], 0.0).then_inc(ident_zero, 1)
            pool.wait_ge(ident_zero, 1)
            pool.affine_select(out=ident[:, :], in_=ident[:, :], compare_op=ALU.not_equal, fill=1.0, base=0,
                               pattern=[[-1, P]], channel_multiplier=1).then_inc(ident_ready, 1)
            for b in range(B):
                pool.memset(proj[:, b, :, G - HEADS:G, DH:DH + 1], 1.0).then_inc(ones_ready, 1)
            pool.memset(shift_l[:, :, :], 1.0).then_inc(zeros_ready, 1)
            pool.memset(mask_b[:, :, S:], 0.0).then_inc(zeros_ready, 1)
            pool.memset(shift_c[:, :, :, :], 0.0).then_inc(zeros_ready, 1)
            pool.wait_ge(zeros_ready, 3)
            pool.memset(shift_c[:, :, :, 32:SH:64], 1.0).then_inc(shift_ready, 1)
            pool.memset(ident_b[:, :], 0.0).then_inc(ident_zero, 1)
            pool.wait_ge(ident_zero, 2)
            pool.affine_select(out=ident_b[:, :], in_=ident_b[:, :], compare_op=ALU.not_equal, fill=1.0, base=0,
                               pattern=[[-1, P]], channel_multiplier=1).then_inc(ident_b_ready, 1)
            pool.memset(logit[:, :, E:], SENTINEL).then_inc(sentinels_ready, 1)
            pool.memset(want[:, :, TOP:], SENTINEL).then_inc(sentinels_ready, 1)

            def background():
                pool.memset(expand[:, :], 0.0).then_inc(expand_ready, 1)
                for i in range(3):
                    pool.wait_ge(expand_ready, i + 1)
                    pool.affine_select(out=expand[:, :], in_=expand[:, :], compare_op=ALU.not_equal, fill=1.0,
                                       base=-E * i, pattern=[[-1, E], [0, F]], channel_multiplier=1).then_inc(expand_ready, 1)
                for src, hi, lo, hi_ready in ((keys, k_hi, k_lo, keys_hi_ready), (values, v_hi, v_lo, values_hi_ready)):
                    pool.wait_ge(hi_ready, EC * P // QUARTER)
                    pool.tensor_tensor(lo[:, :], src[:, :], hi[:, :].bitcast(F32), ALU.subtract).then_inc(split_lo, 1)

            background()

            steps = [0]

            def then(ins):
                steps[0] += 1
                ins.then_inc(pool_step, 1)
                pool.wait_ge(pool_step, steps[0])

            for b in range(B):
                t = slice(BT * b, BT * b + BT)
                pool.wait_ge(gates_ready, b + 1)
                then(pool.tensor_copy(gate_p[:, t, 0, :], gate[:, t, :]))
                then(pool.tensor_tensor(gate_r[:, t, :], gate[:, t, :], gate_p[:, t, 0, :], ALU.subtract))
                then(pool.tensor_copy(gate_p[:, t, 1, :], gate_r[:, t, :]))
                pool.tensor_tensor(gate_p[:, t, 2, :], gate_r[:, t, :], gate_p[:, t, 1, :], ALU.subtract).then_inc(parts_ready, 1)

        @block.vector
        def _(dve):
            steps = [0]

            def then(ins):
                steps[0] += 1
                ins.then_inc(dve_step, 1)
                dve.wait_ge(dve_step, steps[0])

            def newton(y, v, w):
                then(dve.scalar_tensor_tensor(w[:, 1, :], y, -0.5, y, ALU.mult, ALU.mult))
                then(dve.tensor_tensor(w[:, 2, :], w[:, 1, :], v, ALU.mult))
                then(dve.scalar_tensor_tensor(w[:, 3, :], w[:, 2, :], 1.5, y, ALU.add, ALU.mult))

            def stats_in(b):
                dve.wait_ge(in_x[min(b, 2)], 16)
                for t in range(BT):
                    dve.bn_stats(bn_in[:, b, t, :], x[:, BT * b + t, :])
                dve.wait_ge(in_cx[min(b, 2)], 16)
                for t in range(BT):
                    last = dve.bn_stats(bn_in[:, b, BT + t, :], cx[:, BT * b + t, :])
                then(last)
                for t in range(KT):
                    last = dve.bn_aggr(mv_in[:, b, t, :], bn_in[:, b, t, :])
                then(last)
                dve.tensor_scalar(var_in[:, b, 0:BT], mv_in[:, b, 0:BT, 1], 1.0 + LN_EPS, LN_EPS * LN_EPS,
                                  ALU.mult, ALU.add)
                dve.tensor_scalar(var_in[:, b, BT:], mv_in[:, b, BT:, 1], LN_EPS, None, ALU.add).then_inc(var_ready, 1)

            def norm_in(b):
                dve.wait_ge(var_ready, b + 1)
                dve.wait_ge(y0_in, b + 1)
                newton(rs_in[:, b, 0, :], var_in[:, b, :], rs_in[:, b, :, :])
                for t in range(BT):
                    j = BT * b + t
                    dve.tensor_scalar(xn[:, j, :], x[:, j, :], mv_in[:, b, t, 0:1],
                                      rs_in[:, b, 3, t:t + 1], ALU.subtract, ALU.mult).then_inc(xn_ready, 1)
                for t in range(BT):
                    j = BT * b + t
                    dve.tensor_scalar(cn[:, j, :], cx[:, j, :], mv_in[:, b, BT + t, 0:1],
                                      rs_in[:, b, 3, BT + t:BT + t + 1], ALU.subtract, ALU.mult).then_inc(xn_ready, 1)
                if b == 0:
                    dve.wait_ge(in_mask, 16)
                    dve.wait_ge(zeros_ready, 3)
                    dve.tensor_scalar(mask_b[:, :, 0:S], mask_u8[:, :, :], BIG, -BIG, ALU.mult, ALU.add).then_inc(mask_ready, 1)
                    dve.wait_ge(mask_ready, 1)
                    for row in range(32, SH, DH):
                        dve.tensor_copy(shift_l[row:row + 1, :, :], mask_b[row:row + 1, :, :]).then_inc(mask_ready, 1)
                    dve.wait_ge(in_wa, 16)
                    dve.tensor_scalar(gq[:, :], vec(V_QG), float(DH) ** -0.5, None, ALU.mult).then_inc(gq_ready, 1)
                    dve.wait_ge(gq_ready, 1)

            def sum_qk(b):
                dve.wait_ge(squares_ready, 3 * (b + 1))
                then(dve.tensor_reduce(ss[:, b, :], sq[:, b, :, :], mybir.AxisListType.X, ALU.add))
                dve.tensor_scalar(ms[:, b, :], ss[:, b, :], 1.0 / DH, RMS_EPS * RMS_EPS, ALU.mult, ALU.max).then_inc(ms_ready, 1)

            def norm_qk(b):
                dve.wait_ge(ms_ready, b + 1)
                dve.wait_ge(y0_qk, b + 1)
                newton(rs_qk[:, b, 0, :], ms[:, b, :], rs_qk[:, b, :, :])
                for lo, hi, src, n in ((0, KT * HEADS, proj[:, b, :, 2:4, 0:DH], KT),
                                       (KT * HEADS, NR, proj[:, b, BT:, 0:2, 0:DH], BT)):
                    scale = rs_qk[:, b, 3, lo:hi].rearrange("p (t a) -> p t a", t=n).unsqueeze(3)
                    dve.tensor_tensor(qk[:, b, lo:hi, :].rearrange("p (t a) d -> p t a d", t=n), src,
                                      scale.to_broadcast([P, n, HEADS, DH]), ALU.mult).then_inc(qk_ready, 1)

            def turn_qk(b):
                dve.wait_ge(qk_hi_ready, 2 * b + 1)
                dve.scalar_tensor_tensor(kT_lo[:, b, :], bank_of(b, TURN_QK)[:, :], vec(V_KG),
                                         kT_hi[:, b, :].bitcast(F32), ALU.mult, ALU.subtract).then_inc(qk_lo_ready, 1)
                dve.wait_ge(qk_hi_ready, 2 * b + 2)
                dve.scalar_tensor_tensor(qT_lo[:, b, :], bank_of(b, TURN_QK + 1)[:, 0:S], gq[:, :],
                                         qT_hi[:, b, :].bitcast(F32), ALU.mult, ALU.subtract).then_inc(qk_lo_ready, 1)

            def row_max(b):
                for i in range(BT * HEADS):
                    n = BT * HEADS * b + i
                    dve.wait_ge(max_done, n + 1)
                    if n >= 2:
                        dve.wait_ge(max_taken, n - 1)
                    dve.tensor_tensor_reduce(junk[:, n % 2, :], bank_of(b, ROW_MAX + i)[:, :], mask_b[:, b, :], 1.0, SENTINEL,
                                             ALU.add, ALU.max, mx[:, b, i // HEADS, i % HEADS:i % HEADS + 1]).then_inc(max_taken, 1)
                dve.wait_ge(max_taken, BT * HEADS * (b + 1))
                if b == 0:
                    dve.wait_ge(shift_ready, 1)
                dve.tensor_scalar(shift_c[:, b, :, 0:SH:DH], mx[:, b, :, :], -1.0, None, ALU.mult).then_inc(mx_ready, 1)

            def turn_max(b):
                dve.wait_ge(mxT_done, b + 1)
                dve.tensor_copy(shift_r[:, b, :], bank_of(b, TURN_MAX)[0:SH, :].bitcast(BF16)[:, 0:S]).then_inc(shift_set, 1)

            def out_proj(b):
                for t in range(BT):
                    j = BT * b + t
                    dve.wait_ge(out_done_pe, j + 1)
                    last = dve.reciprocal(rsum[:, j, :],
                                          bank_of(b, OUT + t)[:, 0:2 * WOA].rearrange("p (a n) -> p a n", a=HEADS)[:, :, D])
                then(last)
                if b == 0:
                    dve.wait_ge(tanh_ready, 1)
                then(dve.tensor_scalar(rsum_g[:, BT * b:BT * b + BT, :], rsum[:, BT * b:BT * b + BT, :], tanh_g[:, 0:1],
                                       None, ALU.mult))
                for t in range(BT):
                    j = BT * b + t
                    last = dve.scalar_tensor_tensor(x_mid0[:, j, :], bank_of(b, OUT + t)[:, 0:D], rsum_g[:, j, 0:1],
                                                    x[:, j, :], ALU.mult, ALU.add)
                then(last)
                for t in range(BT):
                    j = BT * b + t
                    dve.scalar_tensor_tensor(x_mid[:, j, :], bank_of(b, OUT + t)[:, WOA:WOA + D], rsum_g[:, j, 1:2],
                                             x_mid0[:, j, :], ALU.mult, ALU.add).then_inc(mid_ready, 1)

            def stats_mid(b):
                dve.wait_ge(mid_ready, BT * (b + 1))
                for t in range(BT):
                    last = dve.bn_stats(bn_mid[:, b, t, :], x_mid[:, BT * b + t, :])
                then(last)
                for t in range(BT):
                    last = dve.bn_aggr(mv_mid[:, b, t, :], bn_mid[:, b, t, :])
                then(last)
                dve.tensor_scalar(var_mid[:, b, :], mv_mid[:, b, :, 1], LN_EPS, None, ALU.add).then_inc(var_mid_ready, 1)

            def norm_mid(b):
                dve.wait_ge(var_mid_ready, b + 1)
                dve.wait_ge(y0_mid, b + 1)
                newton(rs_mid[:, b, 0, :], var_mid[:, b, :], rs_mid[:, b, :, :])
                for t in range(BT):
                    j = BT * b + t
                    dve.tensor_scalar(xm[:, j, :], x_mid[:, j, :], mv_mid[:, b, t, 0:1],
                                      rs_mid[:, b, 3, t:t + 1], ALU.subtract, ALU.mult).then_inc(xm_ready, 1)
                if b == 0:
                    dve.wait_ge(in_wb, 16)
                    dve.tensor_copy(sel_hi[:, :], wb[:, B_SEL:B_SEL + E]).then_inc(sel_ready, 1)
                    dve.wait_ge(sel_ready, 1)
                    dve.tensor_tensor(sel_lo[:, :], wb[:, B_SEL:B_SEL + E], sel_hi[:, :].bitcast(F32),
                                      ALU.subtract).then_inc(sel_ready, 1)

            def turn_mid(b):
                dve.wait_ge(xm_hi_ready, b + 1)
                dve.tensor_tensor(xm_lo[:, b, :], bank_of(b, TURN_MID)[:, 0:S], xm_hi[:, b, :].bitcast(F32),
                                  ALU.subtract).then_inc(xm_lo_ready, 1)

            def select(b):
                t = slice(BT * b, BT * b + BT)
                tiles = range(BT * b, BT * b + BT)
                if b == 0:
                    dve.wait_ge(sentinels_ready, 2)
                dve.wait_ge(logit_done, b + 1)
                dve.tensor_scalar(logit[:, t, 0:E], bank_of(b, SELECT)[:, 0:BT * E].rearrange("p (t e) -> p t e", t=BT),
                                  SATURATED, None, ALU.min).then_inc(logit_ready, 1)
                dve.wait_ge(logit_ready, b + 1)
                for j in tiles:
                    last = dve.max(top[:, j, :], logit[:, j, 0:E])
                then(last)
                then(dve.tensor_copy(want[:, t, 0:TOP], top[:, t, 0:TOP]))
                for j in tiles:
                    last = dve.match_replace(left[:, j, :], want[:, j, :], logit[:, j, :], SENTINEL)
                dve.wait_ge(exp_ready, b + 1)
                then(dve.tensor_scalar(one_e[:, t, :], exp_l[:, t, :], 1.0, None, ALU.add))
                then(dve.reciprocal(sig[:, t, :], one_e[:, t, :]))
                dve.scalar_tensor_tensor(gate[:, t, :], left[:, t, 0:E], TAKEN, sig[:, t, :],
                                         ALU.is_lt, ALU.mult).then_inc(gates_ready, 1)

            def up(h, c):
                n = EC * h + c
                dve.wait_ge(relu_ready, n + 1)
                dve.wait_ge(spread_done, n + 1)
                if n >= 3:
                    dve.wait_ge(hid_hi_ready, n - 2)
                    dve.wait_ge(hid_lo_ready, n - 2)
                dve.tensor_tensor(hid[:, n % 3, :], bank[G_BANK][:, :], relu[:, n % 2, :], ALU.mult).then_inc(hid_ready, 1)

            def split(h, c):
                n = EC * h + c
                dve.wait_ge(hid_ready, n + 1)
                dve.wait_ge(hid_hi_ready, n + 1)
                if n >= RING:
                    dve.wait_ge(down_done, n - RING + 1)
                dve.tensor_tensor(hid_lo[:, n % RING, :], hid[:, n % 3, :], hid_hi[:, n % RING, :].bitcast(F32),
                                  ALU.subtract).then_inc(hid_lo_ready, 1)

            def finish(h):
                t = slice(HT * h, HT * h + HT)
                dve.wait_ge(resT_done, h + 1)
                dve.scalar_tensor_tensor(res[:, t, :].rearrange("p t d -> p (t d)"), bank[ACC_BANK[h]][:, :],
                                         tanh_g[:, 1:2], x_mid[:, t, :].rearrange("p t d -> p (t d)"),
                                         ALU.mult, ALU.add).then_inc(res_ready, 1)

            run = {"stats_in": stats_in, "norm_in": norm_in, "sum_qk": sum_qk, "norm_qk": norm_qk,
                   "turn_qk": turn_qk, "stats_mid": stats_mid, "row_max": row_max, "turn_max": turn_max, "split": lambda at: split(*at),
                   "out_proj": out_proj, "norm_mid": norm_mid, "turn_mid": turn_mid, "select": select,
                   "up": lambda at: up(*at), "finish": finish}
            for stage, at in schedule("DVE"):
                if stage in run:
                    run[stage](at)

        @block.scalar
        def _(act):
            steps = [0]

            def start_rsqrt(y0, ln, v, ready):
                steps[0] += 1
                act.activation(ln, v, ACT.Ln).then_inc(act_step, 1)
                act.wait_ge(act_step, steps[0])
                act.activation(y0, ln, ACT.Exp, scale=-0.5).then_inc(ready, 1)

            def stats_in(b):
                if b == 0:
                    act.wait_ge(in_wa, 16)
                    act.activation(tanh_g[:, :], wa[:, A_VEC + V_GX:A_VEC + V_GF + 1], ACT.Tanh).then_inc(tanh_ready, 1)
                    act.preload_act_table_set("natural_log_exp_and_others")
                act.wait_ge(var_ready, b + 1)
                start_rsqrt(rs_in[:, b, 0, :], ln_in[:, b, :], var_in[:, b, :], y0_in)

            def turn_in(b):
                bk = bank_of(b, TURN_IN)
                act.wait_ge(inT_done, b + 1)
                act.activation(xnT[:, b, :], bk[:, 0:S], ACT.Identity, bias=vec(V_LB), scale=vec(V_LG)).then_inc(inT_ready, 1)
                act.activation(cnT[:, b, :], bk[0:DC, S:2 * S], ACT.Identity, bias=vec(V_CB)[0:DC], scale=vec(V_CG)[0:DC]).then_inc(inT_ready, 1)

            def project(b):
                for i in range(3):
                    n = 3 * b + i
                    bk = bank_of(b, PROJECT + i)
                    act.wait_ge(proj_done, n + 1)
                    if i < BT:
                        src = bk[:, 0:G * DH].rearrange("p (g d) -> p g d", g=G)
                        dst = proj[:, b, BT + i, :, 0:DH]
                        act.activation(sq[:, b, HEADS * (BT + i):HEADS * (BT + i + 1), :], src[:, 2:4, :], ACT.Square)
                        act.activation(sq[:, b, HEADS * (KT + i):HEADS * (KT + i + 1), :], src[:, 0:2, :],
                                       ACT.Square).then_inc(squares_ready, 1)
                    else:
                        src = bk[:, :].rearrange("p (t g d) -> p t g d", t=BT, g=4)
                        dst = proj[:, b, 0:BT, 2:G, 0:DH]
                        act.activation(sq[:, b, 0:HEADS * BT, :].rearrange("p (t a) d -> p t a d", t=BT), src[:, :, 0:2, :],
                                       ACT.Square).then_inc(squares_ready, 1)
                    act.activation(dst, src, ACT.Copy).then_inc(proj_ready, 1)

            def split_keys(q):
                if q == 0:
                    act.wait_ge(in_keys, 16)
                act.activation(k_hi[:, QUARTER * q:QUARTER * (q + 1)], keys[:, QUARTER * q:QUARTER * (q + 1)],
                               ACT.Copy).then_inc(keys_hi_ready, 1)

            def split_values(q):
                if q == 0:
                    act.wait_ge(in_values, 16)
                act.activation(v_hi[:, QUARTER * q:QUARTER * (q + 1)], values[:, QUARTER * q:QUARTER * (q + 1)],
                               ACT.Copy).then_inc(values_hi_ready, 1)

            def sum_qk(b):
                act.wait_ge(ms_ready, b + 1)
                start_rsqrt(rs_qk[:, b, 0, :], ln_qk[:, b, :], ms[:, b, :], y0_qk)

            def turn_qk(b):
                if b == 0:
                    act.wait_ge(gq_ready, 1)
                act.wait_ge(qkT_done, 2 * b + 1)
                act.activation(kT_hi[:, b, :], bank_of(b, TURN_QK)[:, :], ACT.Copy, scale=vec(V_KG)).then_inc(qk_hi_ready, 1)
                act.wait_ge(qkT_done, 2 * b + 2)
                act.activation(qT_hi[:, b, :], bank_of(b, TURN_QK + 1)[:, 0:S], ACT.Copy, scale=gq[:, :]).then_inc(qk_hi_ready, 1)

            def weights(b, a):
                n = HEADS * b + a
                for i in range(2):
                    act.wait_ge(score_done, 2 * n + i + 1)
                    if n >= 2 and i == 0:
                        act.wait_ge(attend_done, n - 1)
                    act.activation(prob[:, n % 2, 2 * i:2 * i + 2, :],
                                   bank_of(b, UNITS + 3 * a + i)[:, :].rearrange("p (t s) -> p t s", t=2),
                                   ACT.Exp).then_inc(prob_ready, 1)

            def attend(b, a):
                n = HEADS * b + a
                act.wait_ge(attend_done, n + 1)
                if b >= 2:
                    act.wait_ge(out_done_pe, BT * (b - 1))
                act.activation(oT[:, b % 2, a, :], bank_of(b, UNITS + 3 * a + 2)[0:DH + 1, 0:S], ACT.Copy).then_inc(oT_ready, 1)

            def stats_mid(b):
                act.wait_ge(var_mid_ready, b + 1)
                start_rsqrt(rs_mid[:, b, 0, :], ln_mid[:, b, :], var_mid[:, b, :], y0_mid)

            def turn_mid(b):
                act.wait_ge(xmT_done, b + 1)
                act.activation(xm_hi[:, b, :], bank_of(b, TURN_MID)[:, 0:S], ACT.Copy).then_inc(xm_hi_ready, 1)

            def select(b):
                t = slice(BT * b, BT * b + BT)
                if b == 0:
                    act.wait_ge(split_lo, 1)
                act.wait_ge(logit_ready, b + 1)
                act.activation(exp_l[:, t, :], logit[:, t, 0:E], ACT.Exp, scale=-1.0).then_inc(exp_ready, 1)

            def turn_gates(b):
                act.wait_ge(gateT_done, b + 1)
                act.activation(gateT[:, b, :], bank_of(b, TURN_GATES)[0:3 * E, :].bitcast(BF16)[:, 0:S], ACT.Copy).then_inc(gateT_ready, 1)

            def up(h, c):
                n = EC * h + c
                if n == 0:
                    act.wait_ge(split_lo, 2)
                act.wait_ge(up_done, n + 1)
                if n >= 2:
                    act.wait_ge(hid_ready, n - 1)
                act.activation(relu[:, n % 2, :], bank[H_BANK[n % 2]][:, :], ACT.Relu).then_inc(relu_ready, 1)

            def split(h, c):
                n = EC * h + c
                act.wait_ge(hid_ready, n + 1)
                if n >= RING:
                    act.wait_ge(down_done, n - RING + 1)
                act.activation(hid_hi[:, n % RING, :], hid[:, n % 3, :], ACT.Copy).then_inc(hid_hi_ready, 1)

            def finish(h):
                act.wait_ge(down_done, EC * (h + 1))
                act.activation(yT[:, h, :], bank[ACC_BANK[h]][:, :], ACT.Copy).then_inc(yT_ready, 1)

            run = {"stats_in": stats_in, "turn_in": turn_in, "project": project, "sum_qk": sum_qk, "turn_qk": turn_qk,
                   "split_keys": split_keys, "split_values": split_values, "split": lambda at: split(*at),
                   "weights": lambda at: weights(*at), "attend": lambda at: attend(*at), "stats_mid": stats_mid,
                   "turn_mid": turn_mid, "select": select, "turn_gates": turn_gates,
                   "up": lambda at: up(*at), "finish": finish}
            for stage, at in schedule("ACT"):
                if stage in run:
                    run[stage](at)

        @block.tensor
        def _(pe):
            def half(t, h):
                return t[:, HB * h:HB * h + HB, :].rearrange("p b s -> p (b s)")

            def product(o, lhs, rhs, start, stop):
                (lh, ll), (rh, rl) = lhs, rhs
                pe.matmul(o, ll, rh, start=start, stop=False)
                pe.matmul(o, lh, rl, start=False, stop=False)
                return pe.matmul(o, lh, rh, start=False, stop=stop)

            def keep_warm(n=2):
                for _ in range(n):
                    pe.matmul(bank[7][:, 0:P], ident[:, :], ident[:, :], start=True, stop=True)

            def turn_in(b):
                if b == 0:
                    pe.wait_ge(ident_ready, 1)
                    keep_warm(WARM_UP)
                bk = bank_of(b, TURN_IN)
                pe.wait_ge(xn_ready, KT * b + BT)
                for t in range(BT):
                    pe.transpose(bk[:, P * t:P * t + P], xn[:, BT * b + t, :], ident[:, :])
                pe.wait_ge(xn_ready, KT * (b + 1))
                for t in range(BT):
                    last = pe.transpose(bk[0:DC, S + P * t:S + P * t + P], cn[:, BT * b + t, :], ident[:, :])
                last.then_inc(inT_done, 1)

            def project(b):
                if b == 0:
                    pe.wait_ge(in_wa, 16)
                pe.wait_ge(inT_ready, 2 * (b + 1))
                for i in range(3):
                    bk = bank_of(b, PROJECT + i)
                    if i == 2:
                        pe.wait_ge(proj_ready, 3 * b + 1)
                    if i < BT:
                        last = pe.matmul(bk[:, 0:G * DH], xnT[:, b, P * i:P * i + P], wa[:, A_LAT:A_LAT + G * DH],
                                         start=True, stop=True)
                    else:
                        for t in range(BT):
                            last = pe.matmul(bk[:, 4 * DH * t:4 * DH * (t + 1)], cnT[:, b, P * t:P * t + P],
                                             wa[0:DC, A_CTX:A_CTX + 4 * DH], start=True, stop=True)
                    last.then_inc(proj_done, 1)

            def turn_qk(b):
                pe.wait_ge(proj_ready, 3 * (b + 1))
                for kind, tiles, first in ((0, KT, 0), (1, BT, KT)):
                    pe.wait_ge(qk_ready, 2 * b + kind + 1)
                    for t in range(tiles):
                        src = qk[:, b, HEADS * (first + t):HEADS * (first + t + 1), :].rearrange("p a d -> p (a d)")
                        last = pe.transpose(bank_of(b, TURN_QK + kind)[:, P * t:P * t + P], src, ident[:, :])
                    last.then_inc(qkT_done, 1)

            def row_max(b):
                pe.wait_ge(qk_hi_ready, 2 * (b + 1))
                for i in range(BT * HEADS):
                    n, t, a = BT * HEADS * b + i, i // HEADS, i % HEADS
                    if i < 2:
                        pe.wait_ge(qk_lo_ready, 2 * b + i + 1)
                    else:
                        pe.wait_ge(max_taken, n - 1)
                    rows = slice(DH * a, DH * a + DH)
                    pe.matmul(bank_of(b, ROW_MAX + i)[:, :], qT_hi[rows, b, P * t:P * t + P], kT_hi[rows, b, :],
                              start=True, stop=True).then_inc(max_done, 1)

            def turn_max(b):
                if b == 0:
                    pe.wait_ge(ident_b_ready, 1)
                pe.wait_ge(mx_ready, b + 1)
                bk = bank_of(b, TURN_MAX)[0:SH, :].bitcast(BF16)
                for t in range(BT):
                    last = pe.transpose(bk[:, P * t:P * t + P], shift_c[:, b, t, :], ident_b[:, :])
                last.then_inc(mxT_done, 1)

            def weights(b, a):
                n = HEADS * b + a
                if n == 0:
                    pe.wait_ge(mask_ready, 1 + HEADS)
                if a == 0:
                    pe.wait_ge(shift_set, b + 1)
                rows = slice(DH * a, DH * a + DH)
                for i in range(2):
                    bk = bank_of(b, UNITS + 3 * a + i)
                    if a and i == 0:
                        pe.wait_ge(prob_ready, 2 * n)
                    if a and i == 1:
                        pe.wait_ge(oT_ready, n)
                    for t in range(2 * i, 2 * i + 2):
                        o = bk[:, S * (t % 2):S * (t % 2) + S]
                        keys_t = slice(P * t, P * t + P)
                        pe.matmul(o, shift_l[DH * a:DH * a + 33, b, keys_t], shift_r[DH * a:DH * a + 33, b, :], start=True, stop=False)
                        last = product(o, (kT_hi[rows, b, keys_t], kT_lo[rows, b, keys_t]),
                                       (qT_hi[rows, b, :], qT_lo[rows, b, :]), False, True)
                    last.then_inc(score_done, 1)

            def attend(b, a):
                n = HEADS * b + a
                if n == 0:
                    pe.wait_ge(ones_ready, B)
                pe.wait_ge(prob_ready, 2 * n + 2)
                for t in range(KT):
                    last = pe.matmul(bank_of(b, UNITS + 3 * a + 2)[0:DH + 1, 0:S], proj[:, b, t, 4 + a, :], prob[:, n % 2, t, :],
                                     start=(t == 0), stop=(t == KT - 1))
                last.then_inc(attend_done, 1)

            def out_proj(b):
                if b == 0:
                    pe.wait_ge(in_wb, 16)
                pe.wait_ge(oT_ready, HEADS * (b + 1))
                for t in range(BT):
                    for a in range(HEADS):
                        last = pe.matmul(bank_of(b, OUT + t)[:, WOA * a:WOA * a + WOA], oT[:, b % 2, a, P * t:P * t + P],
                                         wb[0:DH + 1, B_WO + WOA * a:B_WO + WOA * a + WOA], start=True, stop=True)
                    last.then_inc(out_done_pe, 1)

            def turn_mid(b):
                for t in range(BT):
                    j = BT * b + t
                    pe.wait_ge(xm_ready, j + 1)
                    last = pe.transpose(bank_of(b, TURN_MID)[:, P * t:P * t + P], xm[:, j, :], ident[:, :])
                last.then_inc(xmT_done, 1)

            def select(b):
                if b == 0:
                    pe.wait_ge(sel_ready, 2)
                pe.wait_ge(xm_hi_ready, b + 1)
                pe.wait_ge(xm_lo_ready, b + 1)
                for t in range(BT):
                    tt = slice(P * t, P * t + P)
                    last = product(bank_of(b, SELECT)[:, E * t:E * t + E], (xm_hi[:, b, tt], xm_lo[:, b, tt]),
                                   (sel_hi[:, :], sel_lo[:, :]), True, True)
                last.then_inc(logit_done, 1)

            def turn_gates(b):
                pe.wait_ge(parts_ready, b + 1)
                bk = bank_of(b, TURN_GATES)[0:3 * E, :].bitcast(BF16)
                for t in range(BT):
                    src = gate_p[:, BT * b + t, :, :].rearrange("p i e -> p (i e)")
                    last = pe.transpose(bk[:, P * t:P * t + P], src, ident_b[:, :])
                last.then_inc(gateT_done, 1)

            def up(h, c):
                n = EC * h + c
                cc = slice(P * c, P * c + P)
                if n == 0:
                    pe.wait_ge(split_lo, 1)
                    pe.wait_ge(expand_ready, 4)
                if c == 0:
                    pe.wait_ge(gateT_ready, HB * (h + 1))
                if n >= 2:
                    pe.wait_ge(relu_ready, n - 1)
                product(bank[H_BANK[n % 2]][:, :], (k_hi[:, cc], k_lo[:, cc]), (half(xm_hi, h), half(xm_lo, h)),
                        True, True).then_inc(up_done, 1)
                if n >= 1:
                    pe.wait_ge(hid_ready, n)
                pe.matmul(bank[G_BANK][:, :], expand[:, cc], half(gateT, h), start=True, stop=True).then_inc(spread_done, 1)

            def down(h, c):
                n = EC * h + c
                cc = slice(P * c, P * c + P)
                if n == 0:
                    pe.wait_ge(split_lo, 2)
                pe.wait_ge(hid_hi_ready, n + 1)
                pe.wait_ge(hid_lo_ready, n + 1)
                last = product(bank[ACC_BANK[h]][:, :], (v_hi[:, cc], v_lo[:, cc]),
                               (hid_hi[:, n % RING, :], hid_lo[:, n % RING, :]), c == 0, c == EC - 1)
                last.then_inc(down_done, 1)

            def finish(h):
                pe.wait_ge(yT_ready, h + 1)
                for t in range(HT):
                    last = pe.transpose(bank[ACC_BANK[h]][:, P * t:P * t + P], yT[:, h, P * t:P * t + P], ident[:, :])
                last.then_inc(resT_done, 1)

            run = {"keep_warm": lambda at: keep_warm(), "turn_in": turn_in, "project": project, "turn_qk": turn_qk, "row_max": row_max, "turn_max": turn_max,
                   "weights": lambda at: weights(*at), "attend": lambda at: attend(*at), "out_proj": out_proj,
                   "turn_mid": turn_mid, "select": select, "turn_gates": turn_gates,
                   "up": lambda at: up(*at), "down": lambda at: down(*at), "finish": finish}
            for stage, at in schedule("PE"):
                if stage in run:
                    run[stage](at)


def kernel(**inputs):
    import concourse.bacc as bacc
    from concourse.bass_utils import run_bass_kernel_spmd

    a = {k: np.asarray(v) for k, v in inputs.items()}
    f32 = np.float32

    def tiles(t):
        return np.ascontiguousarray(t.reshape(NT, P, t.shape[-1]).transpose(1, 0, 2))

    wa = np.zeros((P, A_COLS), f32)
    wa[:, 0:P] = a["L0_xattn_Wq"].T
    wa[:, P:A_CTX] = a["L0_xattn_Wlkv"].T
    wa[0:DC, A_CTX:A_VEC] = a["L0_xattn_Wkv"].T
    wa[:, A_VEC + V_LG] = a["L0_xattn_ln_l_g"]
    wa[:, A_VEC + V_LB] = a["L0_xattn_ln_l_b"]
    wa[0:DC, A_VEC + V_CG] = a["L0_xattn_ln_x_g"]
    wa[0:DC, A_VEC + V_CB] = a["L0_xattn_ln_x_b"]
    for h in range(HEADS):
        wa[DH * h:DH * h + DH, A_VEC + V_QG] = a["L0_xattn_qn_g"]
        wa[DH * h:DH * h + DH, A_VEC + V_KG] = a["L0_xattn_kn_g"]
    wa[:, A_VEC + V_GX] = a["g_xattn"]
    wa[:, A_VEC + V_GF] = a["g_ffn"]
    wb = np.zeros((P, B_COLS), f32)
    for h in range(HEADS):
        wb[0:DH, WOA * h:WOA * h + D] = a["L0_xattn_Wo"][:, DH * h:DH * h + DH].T
        wb[DH, WOA * h + D] = 1.0
    wb[:, B_SEL:B_SEL + E] = a["L0_ffn_expert_sel"].T
    wb[DH, 0:D] = a["L0_xattn_bo"]

    arrays = {
        "x_in": tiles(a["x"]),
        "ctx_in": tiles(a["ctx_768"]),
        "wa_in": wa,
        "wb_in": wb,
        "mask_in": np.ascontiguousarray(a["mask_BxS2_bk0"]).reshape(1, B * S),
        "keys_in": np.ascontiguousarray(a["L0_ffn_keys"].transpose(1, 0, 2).reshape(D, E * F)),
        "values_in": np.ascontiguousarray(a["L0_ffn_values"].reshape(EC, P, D).transpose(1, 0, 2).reshape(P, EC * D)),
    }
    nc = bacc.Bacc("TRN2", target_bir_lowering=False, num_devices=1)
    args = [nc.dram_tensor(n, v.shape, mybir.dt.from_np(v.dtype), kind="ExternalInput").ap() for n, v in arrays.items()]
    out = nc.dram_tensor("out", (P, NT, D), F32, kind="ExternalOutput").ap()
    gated_block(nc, *args, out)
    got = run_bass_kernel_spmd(nc, [arrays], core_ids=[0]).results[0]["out"]
    return np.ascontiguousarray(got.transpose(1, 0, 2)).reshape(B, S, D)
```

```python
from contextlib import ExitStack

import numpy as np

import concourse.bass as bass
from concourse import mybir

P = 128
ALU = mybir.AluOpType
ACT = mybir.ActivationFunctionType
F32 = mybir.dt.float32
F32R = mybir.dt.float32r
BF16 = mybir.dt.bfloat16
U8 = mybir.dt.uint8

B, S, D, DC = 4, 256, 128, 96
HEADS, DH = 2, 64
E, F = 32, 64
TOP = 4
SH = 97
EC = E * F // P
QUARTER = EC * P // 4
WARM_UP = 12
DOWN = 3
RING = DOWN + 1
NT = B * S // P
BT = S // P
KT = 2 * BT
HALF = 2
HB = B // HALF
HT = NT // HALF
HN = HT * P
G = 6
NR = KT * HEADS + BT * HEADS
LN_EPS = 1e-5
RMS_EPS = 1e-8
BIG = 2.0 ** 100
SATURATED = 16.6355323
SENTINEL = -3.0e38
TAKEN = -1.0e38
WOA = D + 1

PE_ORDER = """
    turn_in 0, project 0, turn_in 1, project 1, turn_qk 0, turn_in 2, row_max 0, project 2, turn_max 0, turn_qk 1,
    weights 0.0, turn_in 3, attend 0.0, weights 0.1, turn_qk 2, row_max 1, project 3, row_max 2, turn_max 1,
    attend 0.1, weights 1.0, turn_max 2, out_proj 0, attend 1.0, turn_qk 3, weights 1.1, weights 2.0, attend 1.1,
    row_max 3, out_proj 1, attend 2.0, turn_max 3, turn_mid 0, weights 2.1, weights 3.0, turn_mid 1, select 0,
    attend 2.1, select 1, attend 3.0, out_proj 2, weights 3.1, turn_gates 0, turn_gates 1, attend 3.1, up 0.0,
    turn_mid 2, out_proj 3, up 0.1, up 0.2, up 0.3, down 0.0, up 0.4, down 0.1, up 0.5, select 2, down 0.2, up 0.6,
    down 0.3, up 0.7, down 0.4, up 0.8, down 0.5, turn_mid 3, up 0.9, down 0.6, up 0.10, down 0.7, up 0.11,
    turn_gates 2, select 3, down 0.8, up 0.12, down 0.9, up 0.13, down 0.10, up 0.14, down 0.11, turn_gates 3,
    up 0.15, down 0.12, up 1.0, down 0.13, down 0.14, up 1.1, down 0.15, up 1.2, up 1.3, finish 0, down 1.0, up 1.4,
    down 1.1, up 1.5, up 1.6, down 1.2, up 1.7, down 1.3, up 1.8, down 1.4, up 1.9, down 1.5, up 1.10, down 1.6,
    up 1.11, up 1.12, down 1.7, up 1.13, down 1.8, up 1.14, down 1.9, up 1.15, down 1.10, down 1.11, down 1.12,
    down 1.13, down 1.14, down 1.15, finish 1
"""
DVE_ORDER = """
    stats_in 0, norm_in 0, stats_in 1, stats_in 2, norm_in 1, sum_qk 0, norm_in 2, norm_qk 0, sum_qk 1, turn_qk 0,
    row_max 0, norm_qk 1, stats_in 3, turn_max 0, norm_in 3, sum_qk 2, turn_qk 1, norm_qk 2, row_max 1, turn_qk 2,
    row_max 2, turn_max 1, sum_qk 3, norm_qk 3, turn_max 2, out_proj 0, stats_mid 0, norm_mid 0, turn_qk 3,
    row_max 3, out_proj 1, stats_mid 1, turn_max 3, turn_mid 0, norm_mid 1, turn_mid 1, select 0, select 1,
    out_proj 2, stats_mid 2, norm_mid 2, up 0.0, out_proj 3, up 0.1, turn_mid 2, split 0.0, up 0.2, split 0.1,
    up 0.3, stats_mid 3, split 0.2, up 0.4, split 0.3, up 0.5, split 0.4, select 2, up 0.6, split 0.5, up 0.7,
    norm_mid 3, split 0.6, up 0.8, split 0.7, up 0.9, split 0.8, turn_mid 3, up 0.10, split 0.9, up 0.11, select 3,
    split 0.10, up 0.12, split 0.11, up 0.13, split 0.12, up 0.14, split 0.13, up 0.15, split 0.14, split 0.15,
    up 1.0, up 1.1, split 1.0, up 1.2, split 1.1, finish 0, up 1.3, split 1.2, up 1.4, split 1.3, up 1.5, split 1.4,
    up 1.6, split 1.5, up 1.7, split 1.6, up 1.8, split 1.7, up 1.9, split 1.8, up 1.10, split 1.9, up 1.11,
    split 1.10, up 1.12, split 1.11, up 1.13, split 1.12, up 1.14, split 1.13, up 1.15, split 1.14, split 1.15,
    finish 1
"""
ACT_ORDER = """
    stats_in 0, turn_in 0, stats_in 1, project 0, stats_in 2, turn_in 1, sum_qk 0, project 1, turn_qk 0, turn_in 2,
    split_keys 0, sum_qk 1, split_keys 1, project 2, stats_in 3, split_values 0, weights 0.0, turn_qk 1, sum_qk 2,
    turn_in 3, attend 0.0, weights 0.1, split_values 1, turn_qk 2, split_values 2, split_values 3, project 3,
    split_keys 2, attend 0.1, sum_qk 3, weights 1.0, split_keys 3, attend 1.0, turn_qk 3, stats_mid 0, weights 1.1,
    weights 2.0, attend 1.1, attend 2.0, stats_mid 1, turn_mid 0, weights 2.1, weights 3.0, turn_mid 1, select 0,
    attend 2.1, select 1, attend 3.0, weights 3.1, turn_gates 0, turn_gates 1, stats_mid 2, attend 3.1, up 0.0,
    turn_mid 2, up 0.1, split 0.0, up 0.2, split 0.1, up 0.3, split 0.2, up 0.4, split 0.3, stats_mid 3, up 0.5,
    split 0.4, select 2, up 0.6, split 0.5, up 0.7, split 0.6, up 0.8, split 0.7, up 0.9, split 0.8, turn_mid 3,
    up 0.10, split 0.9, up 0.11, split 0.10, turn_gates 2, select 3, up 0.12, split 0.11, up 0.13, split 0.12,
    up 0.14, split 0.13, turn_gates 3, up 0.15, split 0.14, split 0.15, up 1.0, up 1.1, split 1.0, finish 0, up 1.2,
    split 1.1, up 1.3, split 1.2, up 1.4, split 1.3, up 1.5, split 1.4, up 1.6, split 1.5, up 1.7, split 1.6,
    up 1.8, split 1.7, up 1.9, split 1.8, up 1.10, split 1.9, up 1.11, split 1.10, up 1.12, split 1.11, up 1.13,
    split 1.12, up 1.14, split 1.13, up 1.15, split 1.14, split 1.15, finish 1
"""

A_LAT, A_CTX = 0, G * DH
A_COLS = A_CTX + 4 * DH
V_LG, V_LB, V_CG, V_CB, V_QG, V_KG, V_GX, V_GF = range(8)
VECS = 8
B_WO, B_SEL = 0, HEADS * WOA
B_COLS = B_SEL + E


def stages(order):
    for entry in order.split(","):
        stage, at = entry.split()
        at = tuple(int(i) for i in at.split("."))
        yield stage, at if len(at) > 1 else at[0]


def gated_block(nc, x_in, ctx_in, wa_in, wb_in, mask_in, keys_in, values_in, out):
    with ExitStack() as ctx:
        def sb(name, shape, dt=F32):
            return ctx.enter_context(nc.sbuf_tensor(name, shape, dt))

        def sem(name):
            return ctx.enter_context(nc.semaphore(name))

        vecs_x = sb("vecs_x", [P, VECS + NT * D])
        x = vecs_x[:, VECS:].rearrange("p (t d) -> p t d", t=NT)
        cx = sb("cx", [P, NT, DC])
        wa = sb("wa", [P, A_COLS])
        wb = sb("wb", [P, B_COLS])
        mask_u8 = sb("mask_u8", [P, B, S], U8)
        keys = sb("keys", [P, EC * P])
        values = sb("values", [P, EC * P])
        ident = sb("ident", [P, P])
        ident_b = sb("ident_b", [P, P], BF16)
        expand = sb("expand", [3 * E, EC * P], BF16)
        shift_l = sb("shift_l", [SH, B, KT * P], BF16)
        shift_r = sb("shift_r", [SH, B, S], BF16)
        mask_b = sb("mask_b", [P, B, KT * P], BF16)
        k_hi, k_lo = sb("k_hi", [P, EC * P], F32R), sb("k_lo", [P, EC * P], F32R)
        v_hi, v_lo = sb("v_hi", [P, EC * P], F32R), sb("v_lo", [P, EC * P], F32R)
        sel_hi, sel_lo = sb("sel_hi", [P, E], F32R), sb("sel_lo", [P, E], F32R)
        tanh_g = sb("tanh_g", [P, 2])
        bn_in = sb("bn_in", [P, B, KT, 6])
        mv_in = sb("mv_in", [P, B, KT, 2])
        var_in = sb("var_in", [P, B, KT])
        ln_in = sb("ln_in", [P, B, KT])
        rs_in = sb("rs_in", [P, B, 4, KT])
        xn = sb("xn", [P, NT, D])
        cn = cx
        xnT = sb("xnT", [P, B, S])
        cnT = sb("cnT", [DC, B, S])
        proj = sb("proj", [P, B, KT, G, DH + 1])
        sq = sb("sq", [P, B, NR, DH])
        ss = sb("ss", [P, B, NR])
        ms = sb("ms", [P, B, NR])
        ln_qk = sb("ln_qk", [P, B, NR])
        rs_qk = sb("rs_qk", [P, B, 4, NR])
        qk = sq
        kT_hi, kT_lo = sb("kT_hi", [P, B, KT * P], F32R), sb("kT_lo", [P, B, KT * P], F32R)
        qT_hi, qT_lo = sb("qT_hi", [P, B, S], F32R), sb("qT_lo", [P, B, S], F32R)
        gq = sb("gq", [P, 1])
        junk = sb("junk", [P, 2, KT * P], BF16)
        mx = sb("mx", [P, B, BT, HEADS])
        shift_c = sb("shift_c", [P, B, BT, SH], BF16)
        prob = sb("prob", [P, 2, KT, S])
        oT = sb("oT", [DH + 1, 2, HEADS, S])
        rsum = sb("rsum", [P, NT, HEADS])
        rsum_g = sb("rsum_g", [P, NT, HEADS])
        x_mid0 = sb("x_mid0", [P, NT, D])
        x_mid = sb("x_mid", [P, NT, D])
        bn_mid = sb("bn_mid", [P, B, BT, 6])
        mv_mid = sb("mv_mid", [P, B, BT, 2])
        var_mid = sb("var_mid", [P, B, BT])
        ln_mid = sb("ln_mid", [P, B, BT])
        rs_mid = sb("rs_mid", [P, B, 4, BT])
        xm = xn
        xm_hi, xm_lo = sb("xm_hi", [P, B, S], F32R), sb("xm_lo", [P, B, S], F32R)
        logit = sb("logit", [P, NT, E + 8])
        top = sb("top", [P, NT, 8])
        want = sb("want", [P, NT, 8])
        left = sb("left", [P, NT, E + 8])
        exp_l = keys[:, 3 * HN:3 * HN + NT * E].rearrange("p (t e) -> p t e", t=NT)
        one_e = keys[:, 3 * HN + NT * E:4 * HN].rearrange("p (t e) -> p t e", t=NT)
        sig = sb("sig", [P, NT, E])
        gate = sb("gate", [P, NT, E])
        gate_r = sb("gate_r", [P, NT, E])
        gate_p = sb("gate_p", [P, NT, 3, E], BF16)
        gateT = sb("gateT", [3 * E, B, S], BF16)
        relu = values[:, 0:2 * HN].rearrange("p (i n) -> p i n", i=2)
        hid = keys[:, 0:3 * HN].rearrange("p (i n) -> p i n", i=3)
        hid_hi, hid_lo = sb("hid_hi", [P, RING, HN], F32R), sb("hid_lo", [P, RING, HN], F32R)
        yT = xn[:, :, :].rearrange("p (h t) d -> p h (t d)", h=HALF)
        res = x_mid0

        bank = [ctx.enter_context(nc.psum_tensor(f"bank{i}", [P, 512], F32)) for i in range(8)]
        H_BANK, ACC_BANK = (0, 1), (3, 7)
        TURN_IN, PROJECT, TURN_QK, ROW_MAX, TURN_MAX, UNITS, OUT, TURN_MID, SELECT, TURN_GATES = 0, 1, 4, 6, 10, 11, 17, 19, 20, 21

        def bank_of(b, use):
            return bank[2 * b + use % 2]


        LOADS = (slice(0, BT), slice(BT, 2 * BT), slice(2 * BT, NT))
        in_x = [sem(f"in_x{i}") for i in range(len(LOADS))]
        in_cx = [sem(f"in_cx{i}") for i in range(len(LOADS))]
        in_wa, in_wb, in_mask = sem("in_wa"), sem("in_wb"), sem("in_mask")
        in_keys, in_values = sem("in_keys"), sem("in_values")
        out_done = sem("out_done")
        ident_zero, ident_ready, ident_b_ready = sem("ident_zero"), sem("ident_ready"), sem("ident_b_ready")
        ones_ready, zeros_ready, shift_ready, expand_ready = sem("ones_ready"), sem("zeros_ready"), sem("shift_ready"), sem("expand_ready")
        sentinels_ready = sem("sentinels_ready")
        split_lo, pool_step, parts_ready = sem("split_lo"), sem("pool_step"), sem("parts_ready")
        mask_ready = sem("mask_ready")
        dve_step = sem("dve_step")
        gq_ready, sel_ready = sem("gq_ready"), sem("sel_ready")
        var_ready, xn_ready = sem("var_ready"), sem("xn_ready")
        ms_ready, qk_ready = sem("ms_ready"), sem("qk_ready")
        qk_lo_ready = sem("qk_lo_ready")
        max_taken, mx_ready, shift_set = sem("max_taken"), sem("mx_ready"), sem("shift_set")
        mid_ready, var_mid_ready, xm_ready, xm_lo_ready = sem("mid_ready"), sem("var_mid_ready"), sem("xm_ready"), sem("xm_lo_ready")
        logit_ready, gates_ready = sem("logit_ready"), sem("gates_ready")
        hid_ready, hid_lo_ready = sem("hid_ready"), sem("hid_lo_ready")
        res_ready = sem("res_ready")
        keys_hi_ready, values_hi_ready = sem("keys_hi_ready"), sem("values_hi_ready")
        squares_ready, hid_hi_ready = sem("squares_ready"), sem("hid_hi_ready")
        tanh_ready, act_step = sem("tanh_ready"), sem("act_step")
        y0_in, y0_qk, y0_mid = sem("y0_in"), sem("y0_qk"), sem("y0_mid")
        inT_ready, proj_ready, qk_hi_ready = sem("inT_ready"), sem("proj_ready"), sem("qk_hi_ready")
        prob_ready, oT_ready = sem("prob_ready"), sem("oT_ready")
        xm_hi_ready, exp_ready, gateT_ready = sem("xm_hi_ready"), sem("exp_ready"), sem("gateT_ready")
        relu_ready, yT_ready = sem("relu_ready"), sem("yT_ready")
        inT_done, proj_done, qkT_done = sem("inT_done"), sem("proj_done"), sem("qkT_done")
        max_done, mxT_done, score_done = sem("max_done"), sem("mxT_done"), sem("score_done")
        attend_done, out_done_pe, xmT_done = sem("attend_done"), sem("out_done_pe"), sem("xmT_done")
        logit_done, gateT_done = sem("logit_done"), sem("gateT_done")
        up_done, spread_done, down_done, resT_done = sem("up_done"), sem("spread_done"), sem("down_done"), sem("resT_done")

        def gates_bank(n):
            return bank[4 if n >= EC and n % 2 else 2]

        def turned(b):
            return bank[3][:, S * b:S * b + S] if b < HB else bank[3 + b][:, 0:S]

        def vec(v):
            return vecs_x[:, v:v + 1]

        block = ctx.enter_context(nc.Block())

        @block.sync
        def _(sp):
            for i, t in enumerate(LOADS):
                cols = slice(VECS + D * t.start if i else 0, VECS + D * t.stop)
                sp.dma_start(vecs_x[:, cols], x_in[:, cols]).then_inc(in_x[i], 16)
                sp.dma_start(cx[:, t, :], ctx_in[:, t, :]).then_inc(in_cx[i], 16)
                if i == 0:
                    sp.dma_start(wa[:, :], wa_in).then_inc(in_wa, 16)
                if i == 1:
                    sp.dma_start(mask_u8[:, :, :].rearrange("p b s -> p (b s)"),
                                 mask_in.to_broadcast([P, B * S])).then_inc(in_mask, 16)
            sp.dma_start(wb[:, :], wb_in).then_inc(in_wb, 16)
            sp.dma_start(keys[:, :], keys_in).then_inc(in_keys, 16)
            sp.dma_start(values[:, :], values_in).then_inc(in_values, 16)
            for b in range(B):
                t = slice(BT * b, BT * b + BT)
                sp.wait_ge(res_ready, b + 1)
                sp.dma_start(out[:, t, :], res[:, t, :]).then_inc(out_done, 16)
            sp.wait_ge(out_done, 16 * B)

        @block.gpsimd
        def _(pool):
            pool.memset(ident[:, :], 0.0).then_inc(ident_zero, 1)
            pool.wait_ge(ident_zero, 1)
            pool.affine_select(out=ident[:, :], in_=ident[:, :], compare_op=ALU.not_equal, fill=1.0, base=0,
                               pattern=[[-1, P]], channel_multiplier=1).then_inc(ident_ready, 1)
            for b in range(B):
                pool.memset(proj[:, b, :, G - HEADS:G, DH:DH + 1], 1.0).then_inc(ones_ready, 1)
            pool.memset(shift_l[:, :, :], 1.0).then_inc(zeros_ready, 1)
            pool.memset(mask_b[:, :, S:], 0.0).then_inc(zeros_ready, 1)
            pool.memset(shift_c[:, :, :, :], 0.0).then_inc(zeros_ready, 1)
            pool.wait_ge(zeros_ready, 3)
            pool.memset(shift_c[:, :, :, 32:SH:64], 1.0).then_inc(shift_ready, 1)
            pool.memset(ident_b[:, :], 0.0).then_inc(ident_zero, 1)
            pool.wait_ge(ident_zero, 2)
            pool.affine_select(out=ident_b[:, :], in_=ident_b[:, :], compare_op=ALU.not_equal, fill=1.0, base=0,
                               pattern=[[-1, P]], channel_multiplier=1).then_inc(ident_b_ready, 1)
            pool.memset(logit[:, :, E:], SENTINEL).then_inc(sentinels_ready, 1)
            pool.memset(want[:, :, TOP:], SENTINEL).then_inc(sentinels_ready, 1)

            pool.wait_ge(in_mask, 16)
            pool.tensor_scalar(mask_b[:, :, 0:S], mask_u8[:, :, :], BIG, -BIG, ALU.mult, ALU.add).then_inc(mask_ready, 1)
            for i, row in enumerate(range(32, SH, DH)):
                pool.wait_ge(mask_ready, i + 1)
                pool.tensor_copy(shift_l[row:row + 1, :, :], mask_b[row:row + 1, :, :]).then_inc(mask_ready, 1)

            def background():
                pool.memset(expand[:, :], 0.0).then_inc(expand_ready, 1)
                for i in range(3):
                    pool.wait_ge(expand_ready, i + 1)
                    pool.affine_select(out=expand[:, :], in_=expand[:, :], compare_op=ALU.not_equal, fill=1.0,
                                       base=-E * i, pattern=[[-1, E], [0, F]], channel_multiplier=1).then_inc(expand_ready, 1)
                for src, hi, lo, hi_ready in ((keys, k_hi, k_lo, keys_hi_ready), (values, v_hi, v_lo, values_hi_ready)):
                    pool.wait_ge(hi_ready, EC * P // QUARTER)
                    pool.tensor_tensor(lo[:, :], src[:, :], hi[:, :].bitcast(F32), ALU.subtract).then_inc(split_lo, 1)

            background()

            steps = [0]

            def then(ins):
                steps[0] += 1
                ins.then_inc(pool_step, 1)
                pool.wait_ge(pool_step, steps[0])

            for b in range(B):
                t = slice(BT * b, BT * b + BT)
                pool.wait_ge(gates_ready, b + 1)
                then(pool.tensor_copy(gate_p[:, t, 0, :], gate[:, t, :]))
                then(pool.tensor_tensor(gate_r[:, t, :], gate[:, t, :], gate_p[:, t, 0, :], ALU.subtract))
                then(pool.tensor_copy(gate_p[:, t, 1, :], gate_r[:, t, :]))
                pool.tensor_tensor(gate_p[:, t, 2, :], gate_r[:, t, :], gate_p[:, t, 1, :], ALU.subtract).then_inc(parts_ready, 1)

        @block.vector
        def _(dve):
            steps = [0]

            def then(ins):
                steps[0] += 1
                ins.then_inc(dve_step, 1)
                dve.wait_ge(dve_step, steps[0])

            def newton(y, v, w):
                then(dve.scalar_tensor_tensor(w[:, 1, :], y, -0.5, y, ALU.mult, ALU.mult))
                then(dve.tensor_tensor(w[:, 2, :], w[:, 1, :], v, ALU.mult))
                then(dve.scalar_tensor_tensor(w[:, 3, :], w[:, 2, :], 1.5, y, ALU.add, ALU.mult))

            def stats_in(b):
                dve.wait_ge(in_x[min(b, 2)], 16)
                for t in range(BT):
                    dve.bn_stats(bn_in[:, b, t, :], x[:, BT * b + t, :])
                dve.wait_ge(in_cx[min(b, 2)], 16)
                for t in range(BT):
                    last = dve.bn_stats(bn_in[:, b, BT + t, :], cx[:, BT * b + t, :])
                then(last)
                for t in range(KT):
                    last = dve.bn_aggr(mv_in[:, b, t, :], bn_in[:, b, t, :])
                then(last)
                dve.tensor_scalar(var_in[:, b, 0:BT], mv_in[:, b, 0:BT, 1], 1.0 + LN_EPS, LN_EPS * LN_EPS,
                                  ALU.mult, ALU.add)
                dve.tensor_scalar(var_in[:, b, BT:], mv_in[:, b, BT:, 1], LN_EPS, None, ALU.add).then_inc(var_ready, 1)

            def norm_in(b):
                dve.wait_ge(var_ready, b + 1)
                dve.wait_ge(y0_in, b + 1)
                newton(rs_in[:, b, 0, :], var_in[:, b, :], rs_in[:, b, :, :])
                for t in range(BT):
                    j = BT * b + t
                    dve.tensor_scalar(xn[:, j, :], x[:, j, :], mv_in[:, b, t, 0:1],
                                      rs_in[:, b, 3, t:t + 1], ALU.subtract, ALU.mult).then_inc(xn_ready, 1)
                for t in range(BT):
                    j = BT * b + t
                    dve.tensor_scalar(cn[:, j, :], cx[:, j, :], mv_in[:, b, BT + t, 0:1],
                                      rs_in[:, b, 3, BT + t:BT + t + 1], ALU.subtract, ALU.mult).then_inc(xn_ready, 1)
                if b == 0:
                    dve.tensor_scalar(gq[:, :], vec(V_QG), float(DH) ** -0.5, None, ALU.mult).then_inc(gq_ready, 1)
                    dve.wait_ge(gq_ready, 1)

            def sum_qk(b):
                dve.wait_ge(squares_ready, 3 * (b + 1))
                then(dve.tensor_reduce(ss[:, b, :], sq[:, b, :, :], mybir.AxisListType.X, ALU.add))
                dve.tensor_scalar(ms[:, b, :], ss[:, b, :], 1.0 / DH, RMS_EPS * RMS_EPS, ALU.mult, ALU.max).then_inc(ms_ready, 1)

            def norm_qk(b):
                dve.wait_ge(ms_ready, b + 1)
                dve.wait_ge(y0_qk, b + 1)
                newton(rs_qk[:, b, 0, :], ms[:, b, :], rs_qk[:, b, :, :])
                for lo, hi, src, n in ((0, KT * HEADS, proj[:, b, :, 2:4, 0:DH], KT),
                                       (KT * HEADS, NR, proj[:, b, BT:, 0:2, 0:DH], BT)):
                    scale = rs_qk[:, b, 3, lo:hi].rearrange("p (t a) -> p t a", t=n).unsqueeze(3)
                    dve.tensor_tensor(qk[:, b, lo:hi, :].rearrange("p (t a) d -> p t a d", t=n), src,
                                      scale.to_broadcast([P, n, HEADS, DH]), ALU.mult).then_inc(qk_ready, 1)

            def turn_qk(b):
                dve.wait_ge(qk_hi_ready, 2 * b + 1)
                dve.scalar_tensor_tensor(kT_lo[:, b, :], bank_of(b, TURN_QK)[:, :], vec(V_KG),
                                         kT_hi[:, b, :].bitcast(F32), ALU.mult, ALU.subtract).then_inc(qk_lo_ready, 1)
                dve.wait_ge(qk_hi_ready, 2 * b + 2)
                dve.scalar_tensor_tensor(qT_lo[:, b, :], bank_of(b, TURN_QK + 1)[:, 0:S], gq[:, :],
                                         qT_hi[:, b, :].bitcast(F32), ALU.mult, ALU.subtract).then_inc(qk_lo_ready, 1)

            def row_max(b):
                if b == 0:
                    dve.wait_ge(mask_ready, 1)
                for i in range(BT * HEADS):
                    n = BT * HEADS * b + i
                    dve.wait_ge(max_done, n + 1)
                    if n >= 2:
                        dve.wait_ge(max_taken, n - 1)
                    dve.tensor_tensor_reduce(junk[:, n % 2, :], bank_of(b, ROW_MAX + i)[:, :], mask_b[:, b, :], 1.0, SENTINEL,
                                             ALU.add, ALU.max, mx[:, b, i // HEADS, i % HEADS:i % HEADS + 1]).then_inc(max_taken, 1)
                dve.wait_ge(max_taken, BT * HEADS * (b + 1))
                if b == 0:
                    dve.wait_ge(shift_ready, 1)
                dve.tensor_scalar(shift_c[:, b, :, 0:SH:DH], mx[:, b, :, :], -1.0, None, ALU.mult).then_inc(mx_ready, 1)

            def turn_max(b):
                dve.wait_ge(mxT_done, b + 1)
                dve.tensor_copy(shift_r[:, b, :], bank_of(b, TURN_MAX)[0:SH, :].bitcast(BF16)[:, 0:S]).then_inc(shift_set, 1)

            def out_proj(b):
                for t in range(BT):
                    j = BT * b + t
                    dve.wait_ge(out_done_pe, j + 1)
                    last = dve.reciprocal(rsum[:, j, :],
                                          bank_of(b, OUT + t)[:, 0:2 * WOA].rearrange("p (a n) -> p a n", a=HEADS)[:, :, D])
                then(last)
                if b == 0:
                    dve.wait_ge(tanh_ready, 1)
                then(dve.tensor_scalar(rsum_g[:, BT * b:BT * b + BT, :], rsum[:, BT * b:BT * b + BT, :], tanh_g[:, 0:1],
                                       None, ALU.mult))
                for t in range(BT):
                    j = BT * b + t
                    last = dve.scalar_tensor_tensor(x_mid0[:, j, :], bank_of(b, OUT + t)[:, 0:D], rsum_g[:, j, 0:1],
                                                    x[:, j, :], ALU.mult, ALU.add)
                then(last)
                for t in range(BT):
                    j = BT * b + t
                    dve.scalar_tensor_tensor(x_mid[:, j, :], bank_of(b, OUT + t)[:, WOA:WOA + D], rsum_g[:, j, 1:2],
                                             x_mid0[:, j, :], ALU.mult, ALU.add).then_inc(mid_ready, 1)

            def stats_mid(b):
                dve.wait_ge(mid_ready, BT * (b + 1))
                for t in range(BT):
                    last = dve.bn_stats(bn_mid[:, b, t, :], x_mid[:, BT * b + t, :])
                then(last)
                for t in range(BT):
                    last = dve.bn_aggr(mv_mid[:, b, t, :], bn_mid[:, b, t, :])
                then(last)
                dve.tensor_scalar(var_mid[:, b, :], mv_mid[:, b, :, 1], LN_EPS, None, ALU.add).then_inc(var_mid_ready, 1)

            def norm_mid(b):
                dve.wait_ge(var_mid_ready, b + 1)
                dve.wait_ge(y0_mid, b + 1)
                newton(rs_mid[:, b, 0, :], var_mid[:, b, :], rs_mid[:, b, :, :])
                for t in range(BT):
                    j = BT * b + t
                    dve.tensor_scalar(xm[:, j, :], x_mid[:, j, :], mv_mid[:, b, t, 0:1],
                                      rs_mid[:, b, 3, t:t + 1], ALU.subtract, ALU.mult).then_inc(xm_ready, 1)
                if b == 0:
                    dve.wait_ge(in_wb, 16)
                    dve.tensor_copy(sel_hi[:, :], wb[:, B_SEL:B_SEL + E]).then_inc(sel_ready, 1)
                    dve.wait_ge(sel_ready, 1)
                    dve.tensor_tensor(sel_lo[:, :], wb[:, B_SEL:B_SEL + E], sel_hi[:, :].bitcast(F32),
                                      ALU.subtract).then_inc(sel_ready, 1)

            def turn_mid(b):
                dve.wait_ge(xm_hi_ready, b + 1)
                dve.tensor_tensor(xm_lo[:, b, :], bank_of(b, TURN_MID)[:, 0:S], xm_hi[:, b, :].bitcast(F32),
                                  ALU.subtract).then_inc(xm_lo_ready, 1)

            def select(b):
                t = slice(BT * b, BT * b + BT)
                tiles = range(BT * b, BT * b + BT)
                if b == 0:
                    dve.wait_ge(sentinels_ready, 2)
                dve.wait_ge(logit_done, b + 1)
                dve.tensor_scalar(logit[:, t, 0:E], bank_of(b, SELECT)[:, 0:BT * E].rearrange("p (t e) -> p t e", t=BT),
                                  SATURATED, None, ALU.min).then_inc(logit_ready, 1)
                dve.wait_ge(logit_ready, b + 1)
                for j in tiles:
                    last = dve.max(top[:, j, :], logit[:, j, 0:E])
                then(last)
                then(dve.tensor_copy(want[:, t, 0:TOP], top[:, t, 0:TOP]))
                for j in tiles:
                    last = dve.match_replace(left[:, j, :], want[:, j, :], logit[:, j, :], SENTINEL)
                dve.wait_ge(exp_ready, b + 1)
                then(dve.tensor_scalar(one_e[:, t, :], exp_l[:, t, :], 1.0, None, ALU.add))
                then(dve.reciprocal(sig[:, t, :], one_e[:, t, :]))
                dve.scalar_tensor_tensor(gate[:, t, :], left[:, t, 0:E], TAKEN, sig[:, t, :],
                                         ALU.is_lt, ALU.mult).then_inc(gates_ready, 1)

            def up(h, c):
                n = EC * h + c
                dve.wait_ge(relu_ready, n + 1)
                dve.wait_ge(spread_done, n + 1)
                if n >= 3:
                    dve.wait_ge(hid_hi_ready, n - 2)
                    dve.wait_ge(hid_lo_ready, n - 2)
                dve.tensor_tensor(hid[:, n % 3, :], gates_bank(n)[:, :], relu[:, n % 2, :], ALU.mult).then_inc(hid_ready, 1)

            def split(h, c):
                n = EC * h + c
                dve.wait_ge(hid_ready, n + 1)
                dve.wait_ge(hid_hi_ready, n + 1)
                if n >= RING:
                    dve.wait_ge(down_done, n - RING + 1)
                dve.tensor_tensor(hid_lo[:, n % RING, :], hid[:, n % 3, :], hid_hi[:, n % RING, :].bitcast(F32),
                                  ALU.subtract).then_inc(hid_lo_ready, 1)

            def finish(h):
                for b in range(HB * h, HB * h + HB):
                    t = slice(BT * b, BT * b + BT)
                    dve.wait_ge(resT_done, HB if h == 0 else b + 1)
                    dve.scalar_tensor_tensor(res[:, t, :].rearrange("p t d -> p (t d)"), turned(b),
                                             tanh_g[:, 1:2], x_mid[:, t, :].rearrange("p t d -> p (t d)"),
                                             ALU.mult, ALU.add).then_inc(res_ready, 1)

            run = {"stats_in": stats_in, "norm_in": norm_in, "sum_qk": sum_qk, "norm_qk": norm_qk,
                   "turn_qk": turn_qk, "stats_mid": stats_mid, "row_max": row_max, "turn_max": turn_max, "split": lambda at: split(*at),
                   "out_proj": out_proj, "norm_mid": norm_mid, "turn_mid": turn_mid, "select": select,
                   "up": lambda at: up(*at), "finish": finish}
            for stage, at in stages(DVE_ORDER):
                run[stage](at)

        @block.scalar
        def _(act):
            steps = [0]

            def start_rsqrt(y0, ln, v, ready):
                steps[0] += 1
                act.activation(ln, v, ACT.Ln).then_inc(act_step, 1)
                act.wait_ge(act_step, steps[0])
                act.activation(y0, ln, ACT.Exp, scale=-0.5).then_inc(ready, 1)

            def stats_in(b):
                if b == 0:
                    act.wait_ge(in_x[0], 16)
                    act.activation(tanh_g[:, :], vecs_x[:, V_GX:V_GF + 1], ACT.Tanh).then_inc(tanh_ready, 1)
                    act.preload_act_table_set("natural_log_exp_and_others")
                act.wait_ge(var_ready, b + 1)
                start_rsqrt(rs_in[:, b, 0, :], ln_in[:, b, :], var_in[:, b, :], y0_in)

            def turn_in(b):
                bk = bank_of(b, TURN_IN)
                act.wait_ge(inT_done, b + 1)
                act.activation(xnT[:, b, :], bk[:, 0:S], ACT.Identity, bias=vec(V_LB), scale=vec(V_LG)).then_inc(inT_ready, 1)
                act.activation(cnT[:, b, :], bk[0:DC, S:2 * S], ACT.Identity, bias=vec(V_CB)[0:DC], scale=vec(V_CG)[0:DC]).then_inc(inT_ready, 1)

            def project(b):
                for i in range(3):
                    n = 3 * b + i
                    bk = bank_of(b, PROJECT + i)
                    act.wait_ge(proj_done, n + 1)
                    if i < BT:
                        src = bk[:, 0:G * DH].rearrange("p (g d) -> p g d", g=G)
                        dst = proj[:, b, BT + i, :, 0:DH]
                        act.activation(sq[:, b, HEADS * (BT + i):HEADS * (BT + i + 1), :], src[:, 2:4, :], ACT.Square)
                        act.activation(sq[:, b, HEADS * (KT + i):HEADS * (KT + i + 1), :], src[:, 0:2, :],
                                       ACT.Square).then_inc(squares_ready, 1)
                    else:
                        src = bk[:, :].rearrange("p (t g d) -> p t g d", t=BT, g=4)
                        dst = proj[:, b, 0:BT, 2:G, 0:DH]
                        act.activation(sq[:, b, 0:HEADS * BT, :].rearrange("p (t a) d -> p t a d", t=BT), src[:, :, 0:2, :],
                                       ACT.Square).then_inc(squares_ready, 1)
                    act.activation(dst, src, ACT.Copy).then_inc(proj_ready, 1)

            def split_keys(q):
                if q == 0:
                    act.wait_ge(in_keys, 16)
                act.activation(k_hi[:, QUARTER * q:QUARTER * (q + 1)], keys[:, QUARTER * q:QUARTER * (q + 1)],
                               ACT.Copy).then_inc(keys_hi_ready, 1)

            def split_values(q):
                if q == 0:
                    act.wait_ge(in_values, 16)
                act.activation(v_hi[:, QUARTER * q:QUARTER * (q + 1)], values[:, QUARTER * q:QUARTER * (q + 1)],
                               ACT.Copy).then_inc(values_hi_ready, 1)

            def sum_qk(b):
                act.wait_ge(ms_ready, b + 1)
                start_rsqrt(rs_qk[:, b, 0, :], ln_qk[:, b, :], ms[:, b, :], y0_qk)

            def turn_qk(b):
                if b == 0:
                    act.wait_ge(gq_ready, 1)
                act.wait_ge(qkT_done, 2 * b + 1)
                act.activation(kT_hi[:, b, :], bank_of(b, TURN_QK)[:, :], ACT.Copy, scale=vec(V_KG)).then_inc(qk_hi_ready, 1)
                act.wait_ge(qkT_done, 2 * b + 2)
                act.activation(qT_hi[:, b, :], bank_of(b, TURN_QK + 1)[:, 0:S], ACT.Copy, scale=gq[:, :]).then_inc(qk_hi_ready, 1)

            def weights(b, a):
                n = HEADS * b + a
                for i in range(2):
                    act.wait_ge(score_done, 2 * n + i + 1)
                    if n >= 2 and i == 0:
                        act.wait_ge(attend_done, n - 1)
                    act.activation(prob[:, n % 2, 2 * i:2 * i + 2, :],
                                   bank_of(b, UNITS + 3 * a + i)[:, :].rearrange("p (t s) -> p t s", t=2),
                                   ACT.Exp).then_inc(prob_ready, 1)

            def attend(b, a):
                n = HEADS * b + a
                act.wait_ge(attend_done, n + 1)
                if b >= 2:
                    act.wait_ge(out_done_pe, BT * (b - 1))
                act.activation(oT[:, b % 2, a, :], bank_of(b, UNITS + 3 * a + 2)[0:DH + 1, 0:S], ACT.Copy).then_inc(oT_ready, 1)

            def stats_mid(b):
                act.wait_ge(var_mid_ready, b + 1)
                start_rsqrt(rs_mid[:, b, 0, :], ln_mid[:, b, :], var_mid[:, b, :], y0_mid)

            def turn_mid(b):
                act.wait_ge(xmT_done, b + 1)
                act.activation(xm_hi[:, b, :], bank_of(b, TURN_MID)[:, 0:S], ACT.Copy).then_inc(xm_hi_ready, 1)

            def select(b):
                t = slice(BT * b, BT * b + BT)
                if b == 0:
                    act.wait_ge(split_lo, 1)
                act.wait_ge(logit_ready, b + 1)
                act.activation(exp_l[:, t, :], logit[:, t, 0:E], ACT.Exp, scale=-1.0).then_inc(exp_ready, 1)

            def turn_gates(b):
                act.wait_ge(gateT_done, b + 1)
                act.activation(gateT[:, b, :], bank_of(b, TURN_GATES)[0:3 * E, :].bitcast(BF16)[:, 0:S], ACT.Copy).then_inc(gateT_ready, 1)

            def up(h, c):
                n = EC * h + c
                if n == 0:
                    act.wait_ge(split_lo, 2)
                act.wait_ge(up_done, n + 1)
                if n >= 2:
                    act.wait_ge(hid_ready, n - 1)
                act.activation(relu[:, n % 2, :], bank[H_BANK[n % 2]][:, :], ACT.Relu).then_inc(relu_ready, 1)

            def split(h, c):
                n = EC * h + c
                act.wait_ge(hid_ready, n + 1)
                if n >= RING:
                    act.wait_ge(down_done, n - RING + 1)
                act.activation(hid_hi[:, n % RING, :], hid[:, n % 3, :], ACT.Copy).then_inc(hid_hi_ready, 1)

            def finish(h):
                act.wait_ge(down_done, EC * (h + 1))
                for i in range(HB):
                    part = slice(S * i, S * i + S)
                    act.activation(yT[:, h, part], bank[ACC_BANK[h]][:, part], ACT.Copy).then_inc(yT_ready, 1)

            run = {"stats_in": stats_in, "turn_in": turn_in, "project": project, "sum_qk": sum_qk, "turn_qk": turn_qk,
                   "split_keys": split_keys, "split_values": split_values, "split": lambda at: split(*at),
                   "weights": lambda at: weights(*at), "attend": lambda at: attend(*at), "stats_mid": stats_mid,
                   "turn_mid": turn_mid, "select": select, "turn_gates": turn_gates,
                   "up": lambda at: up(*at), "finish": finish}
            for stage, at in stages(ACT_ORDER):
                run[stage](at)

        @block.tensor
        def _(pe):
            def half(t, h):
                return t[:, HB * h:HB * h + HB, :].rearrange("p b s -> p (b s)")

            def product(o, lhs, rhs, start, stop):
                (lh, ll), (rh, rl) = lhs, rhs
                pe.matmul(o, ll, rh, start=start, stop=False)
                pe.matmul(o, lh, rl, start=False, stop=False)
                return pe.matmul(o, lh, rh, start=False, stop=stop)

            def turn_in(b):
                if b == 0:
                    pe.wait_ge(ident_ready, 1)
                    for _ in range(WARM_UP):
                        pe.matmul(bank[7][:, 0:P], ident[:, :], ident[:, :], start=True, stop=True)
                bk = bank_of(b, TURN_IN)
                pe.wait_ge(xn_ready, KT * b + BT)
                for t in range(BT):
                    pe.transpose(bk[:, P * t:P * t + P], xn[:, BT * b + t, :], ident[:, :])
                pe.wait_ge(xn_ready, KT * (b + 1))
                for t in range(BT):
                    last = pe.transpose(bk[0:DC, S + P * t:S + P * t + P], cn[:, BT * b + t, :], ident[:, :])
                last.then_inc(inT_done, 1)

            def project(b):
                if b == 0:
                    pe.wait_ge(in_wa, 16)
                for i in range(3):
                    if i < 2:
                        pe.wait_ge(inT_ready, 2 * b + i + 1)
                    bk = bank_of(b, PROJECT + i)
                    if i == 2:
                        pe.wait_ge(proj_ready, 3 * b + 1)
                    if i < BT:
                        last = pe.matmul(bk[:, 0:G * DH], xnT[:, b, P * i:P * i + P], wa[:, A_LAT:A_LAT + G * DH],
                                         start=True, stop=True)
                    else:
                        for t in range(BT):
                            last = pe.matmul(bk[:, 4 * DH * t:4 * DH * (t + 1)], cnT[:, b, P * t:P * t + P],
                                             wa[0:DC, A_CTX:A_CTX + 4 * DH], start=True, stop=True)
                    last.then_inc(proj_done, 1)

            def turn_qk(b):
                pe.wait_ge(proj_ready, 3 * (b + 1))
                for kind, tiles, first in ((0, KT, 0), (1, BT, KT)):
                    pe.wait_ge(qk_ready, 2 * b + kind + 1)
                    for t in range(tiles):
                        src = qk[:, b, HEADS * (first + t):HEADS * (first + t + 1), :].rearrange("p a d -> p (a d)")
                        last = pe.transpose(bank_of(b, TURN_QK + kind)[:, P * t:P * t + P], src, ident[:, :])
                    last.then_inc(qkT_done, 1)

            def row_max(b):
                pe.wait_ge(qk_hi_ready, 2 * (b + 1))
                for i in range(BT * HEADS):
                    n, t, a = BT * HEADS * b + i, i // HEADS, i % HEADS
                    if i < 2:
                        pe.wait_ge(qk_lo_ready, 2 * b + i + 1)
                    else:
                        pe.wait_ge(max_taken, n - 1)
                    rows = slice(DH * a, DH * a + DH)
                    pe.matmul(bank_of(b, ROW_MAX + i)[:, :], qT_hi[rows, b, P * t:P * t + P], kT_hi[rows, b, :],
                              start=True, stop=True).then_inc(max_done, 1)

            def turn_max(b):
                if b == 0:
                    pe.wait_ge(ident_b_ready, 1)
                pe.wait_ge(mx_ready, b + 1)
                bk = bank_of(b, TURN_MAX)[0:SH, :].bitcast(BF16)
                for t in range(BT):
                    last = pe.transpose(bk[:, P * t:P * t + P], shift_c[:, b, t, :], ident_b[:, :])
                last.then_inc(mxT_done, 1)

            def weights(b, a):
                n = HEADS * b + a
                if n == 0:
                    pe.wait_ge(mask_ready, 1 + HEADS)
                if a == 0:
                    pe.wait_ge(shift_set, b + 1)
                rows = slice(DH * a, DH * a + DH)
                for i in range(2):
                    bk = bank_of(b, UNITS + 3 * a + i)
                    if a and i == 0:
                        pe.wait_ge(prob_ready, 2 * n)
                    if a and i == 1:
                        pe.wait_ge(oT_ready, n)
                    for t in range(2 * i, 2 * i + 2):
                        o = bk[:, S * (t % 2):S * (t % 2) + S]
                        keys_t = slice(P * t, P * t + P)
                        pe.matmul(o, shift_l[DH * a:DH * a + 33, b, keys_t], shift_r[DH * a:DH * a + 33, b, :], start=True, stop=False)
                        last = product(o, (kT_hi[rows, b, keys_t], kT_lo[rows, b, keys_t]),
                                       (qT_hi[rows, b, :], qT_lo[rows, b, :]), False, True)
                    last.then_inc(score_done, 1)

            def attend(b, a):
                n = HEADS * b + a
                if n == 0:
                    pe.wait_ge(ones_ready, B)
                pe.wait_ge(prob_ready, 2 * n + 2)
                for t in range(KT):
                    last = pe.matmul(bank_of(b, UNITS + 3 * a + 2)[0:DH + 1, 0:S], proj[:, b, t, 4 + a, :], prob[:, n % 2, t, :],
                                     start=(t == 0), stop=(t == KT - 1))
                last.then_inc(attend_done, 1)

            def out_proj(b):
                if b == 0:
                    pe.wait_ge(in_wb, 16)
                pe.wait_ge(oT_ready, HEADS * (b + 1))
                for t in range(BT):
                    for a in range(HEADS):
                        last = pe.matmul(bank_of(b, OUT + t)[:, WOA * a:WOA * a + WOA], oT[:, b % 2, a, P * t:P * t + P],
                                         wb[0:DH + 1, B_WO + WOA * a:B_WO + WOA * a + WOA], start=True, stop=True)
                    last.then_inc(out_done_pe, 1)

            def turn_mid(b):
                for t in range(BT):
                    j = BT * b + t
                    pe.wait_ge(xm_ready, j + 1)
                    last = pe.transpose(bank_of(b, TURN_MID)[:, P * t:P * t + P], xm[:, j, :], ident[:, :])
                last.then_inc(xmT_done, 1)

            def select(b):
                if b == 0:
                    pe.wait_ge(sel_ready, 2)
                pe.wait_ge(xm_hi_ready, b + 1)
                pe.wait_ge(xm_lo_ready, b + 1)
                for t in range(BT):
                    tt = slice(P * t, P * t + P)
                    last = product(bank_of(b, SELECT)[:, E * t:E * t + E], (xm_hi[:, b, tt], xm_lo[:, b, tt]),
                                   (sel_hi[:, :], sel_lo[:, :]), True, True)
                last.then_inc(logit_done, 1)

            def turn_gates(b):
                pe.wait_ge(parts_ready, b + 1)
                bk = bank_of(b, TURN_GATES)[0:3 * E, :].bitcast(BF16)
                for t in range(BT):
                    src = gate_p[:, BT * b + t, :, :].rearrange("p i e -> p (i e)")
                    last = pe.transpose(bk[:, P * t:P * t + P], src, ident_b[:, :])
                last.then_inc(gateT_done, 1)

            def up(h, c):
                n = EC * h + c
                cc = slice(P * c, P * c + P)
                if n == 0:
                    pe.wait_ge(split_lo, 1)
                    pe.wait_ge(expand_ready, 4)
                if c == 0:
                    pe.wait_ge(gateT_ready, HB * (h + 1))
                if n >= 2:
                    pe.wait_ge(relu_ready, n - 1)
                product(bank[H_BANK[n % 2]][:, :], (k_hi[:, cc], k_lo[:, cc]), (half(xm_hi, h), half(xm_lo, h)),
                        True, True).then_inc(up_done, 1)
                if n >= 1:
                    pe.wait_ge(hid_ready, n - 1 if n > EC + 1 else n)
                pe.matmul(gates_bank(n)[:, :], expand[:, cc], half(gateT, h), start=True, stop=True).then_inc(spread_done, 1)

            def down(h, c):
                n = EC * h + c
                cc = slice(P * c, P * c + P)
                if n == 0:
                    pe.wait_ge(split_lo, 2)
                pe.wait_ge(hid_hi_ready, n + 1)
                pe.wait_ge(hid_lo_ready, n + 1)
                last = product(bank[ACC_BANK[h]][:, :], (v_hi[:, cc], v_lo[:, cc]),
                               (hid_hi[:, n % RING, :], hid_lo[:, n % RING, :]), c == 0, c == EC - 1)
                last.then_inc(down_done, 1)

            def finish(h):
                for b in range(HB * h, HB * h + HB):
                    pe.wait_ge(yT_ready, HB if h == 0 else b + 1)
                    for t in range(BT):
                        col = S * (b % HB) + P * t
                        last = pe.transpose(turned(b)[:, P * t:P * t + P], yT[:, h, col:col + P], ident[:, :])
                    last.then_inc(resT_done, 1)

            run = {"turn_in": turn_in, "project": project, "turn_qk": turn_qk, "row_max": row_max, "turn_max": turn_max,
                   "weights": lambda at: weights(*at), "attend": lambda at: attend(*at), "out_proj": out_proj,
                   "turn_mid": turn_mid, "select": select, "turn_gates": turn_gates,
                   "up": lambda at: up(*at), "down": lambda at: down(*at), "finish": finish}
            for stage, at in stages(PE_ORDER):
                run[stage](at)


def kernel(**inputs):
    import concourse.bacc as bacc
    from concourse.bass_utils import run_bass_kernel_spmd

    a = {k: np.asarray(v) for k, v in inputs.items()}
    f32 = np.float32

    def tiles(t):
        return np.ascontiguousarray(t.reshape(NT, P, t.shape[-1]).transpose(1, 0, 2))

    vecs = np.zeros((P, VECS), f32)
    vecs[:, V_LG] = a["L0_xattn_ln_l_g"]
    vecs[:, V_LB] = a["L0_xattn_ln_l_b"]
    vecs[0:DC, V_CG] = a["L0_xattn_ln_x_g"]
    vecs[0:DC, V_CB] = a["L0_xattn_ln_x_b"]
    for h in range(HEADS):
        vecs[DH * h:DH * h + DH, V_QG] = a["L0_xattn_qn_g"]
        vecs[DH * h:DH * h + DH, V_KG] = a["L0_xattn_kn_g"]
    vecs[:, V_GX] = a["g_xattn"]
    vecs[:, V_GF] = a["g_ffn"]
    wa = np.zeros((P, A_COLS), f32)
    wa[:, 0:P] = a["L0_xattn_Wq"].T
    wa[:, P:A_CTX] = a["L0_xattn_Wlkv"].T
    wa[0:DC, A_CTX:A_COLS] = a["L0_xattn_Wkv"].T
    wb = np.zeros((P, B_COLS), f32)
    for h in range(HEADS):
        wb[0:DH, WOA * h:WOA * h + D] = a["L0_xattn_Wo"][:, DH * h:DH * h + DH].T
        wb[DH, WOA * h + D] = 1.0
    wb[:, B_SEL:B_SEL + E] = a["L0_ffn_expert_sel"].T
    wb[DH, 0:D] = a["L0_xattn_bo"]

    arrays = {
        "x_in": np.concatenate([vecs, tiles(a["x"]).reshape(P, NT * D)], axis=1),
        "ctx_in": tiles(a["ctx_768"]),
        "wa_in": wa,
        "wb_in": wb,
        "mask_in": np.ascontiguousarray(a["mask_BxS2_bk0"]).reshape(1, B * S),
        "keys_in": np.ascontiguousarray(a["L0_ffn_keys"].transpose(1, 0, 2).reshape(D, E * F)),
        "values_in": np.ascontiguousarray(a["L0_ffn_values"].reshape(EC, P, D).transpose(1, 0, 2).reshape(P, EC * D)),
    }
    nc = bacc.Bacc("TRN2", target_bir_lowering=False, num_devices=1)
    args = [nc.dram_tensor(n, v.shape, mybir.dt.from_np(v.dtype), kind="ExternalInput").ap() for n, v in arrays.items()]
    out = nc.dram_tensor("out", (P, NT, D), F32, kind="ExternalOutput").ap()
    gated_block(nc, *args, out)
    got = run_bass_kernel_spmd(nc, [arrays], core_ids=[0]).results[0]["out"]
    return np.ascontiguousarray(got.transpose(1, 0, 2)).reshape(B, S, D)
```
